# Optimizing a Trainium2 kernel written in Bass

```python
import numpy as np
import jax
import jax.numpy as jnp

def _softmax(x, axis=-1):
    return jax.nn.softmax(x, axis=axis)

def _gelu(x):
    return jax.nn.gelu(x, approximate=True)

def _silu(x):
    return jax.nn.silu(x)

def _sigmoid(x):
    return jax.nn.sigmoid(x)

def _layernorm(x, axis=-1, eps=1e-05):
    m = jnp.mean(x, axis=axis, keepdims=True)
    v = jnp.var(x, axis=axis, keepdims=True)
    return (x - m) / jnp.sqrt(v + eps)

def _scatter_add(tgt, idx, src, axis=0):
    return tgt.at[idx].add(src)

def _segment_sum(src, seg, n):
    return jax.ops.segment_sum(src, seg, n)
kernel_name = 'mk_cond_resid_d4_seqx_r8_183e9a'

def setup_inputs(seed: int=0):
    np.random.seed(seed)
    _w = jnp.asarray

    def _rec_inputs():
        import jax
        import jax.numpy as jnp
        _rk = jax.random.key(seed)
        x = -0.0005207 + 1.001 * jax.random.normal(jax.random.fold_in(_rk, 1), (8, 128, 512), jnp.float32)
        _lenS = 128 - jax.random.randint(jax.random.fold_in(_rk, 7), (8,), 0, max(1, 128 // 4) + 1, jnp.int32)
        _lenS2 = 128 - jax.random.randint(jax.random.fold_in(_rk, 8), (8,), 0, max(1, 128 // 4) + 1, jnp.int32)
        itok_Bx16_0_63 = jax.random.randint(jax.random.fold_in(_rk, 11), (8, 16), 0, 64, jnp.int32)
        itok_B_207_1644 = jax.random.randint(jax.random.fold_in(_rk, 12), (8,), 207, 1645, jnp.int32)
        itok_B_0_4 = jax.random.randint(jax.random.fold_in(_rk, 13), (8,), 0, 5, jnp.int32)
        itok_B_0_7 = jax.random.randint(jax.random.fold_in(_rk, 14), (8,), 0, 8, jnp.int32)
        itok_B_2_6 = jax.random.randint(jax.random.fold_in(_rk, 15), (8,), 2, 7, jnp.int32)
        return (x, itok_Bx16_0_63, itok_B_207_1644, itok_B_0_4, itok_B_0_7, itok_B_2_6)
    x, itok_Bx16_0_63, itok_B_207_1644, itok_B_0_4, itok_B_0_7, itok_B_2_6 = _rec_inputs()

    def _L0_cond_setup():
        import jax, jax.numpy as jnp
        import numpy as np
        B, S, HID = (4, 128, 512)
        D, HQ, HK = (128, 32, 8)
        PAGES, PSIZE, NPP = (64, 32, 16)
        THETA = 10000.0
        EPS = 1e-06
        SCALE = 1.0 / float(np.sqrt(D))

        def _rmsnorm(t, w):
            var = jnp.mean(t * t, axis=-1, keepdims=True)
            return t * jax.lax.rsqrt(var + EPS) * w

        def _rope(t, pos):
            inv_freq = 1.0 / THETA ** (jnp.arange(0, D, 2, dtype=jnp.float32) / D)
            freqs = pos[..., None].astype(jnp.float32) * inv_freq
            cos = jnp.cos(freqs)[:, :, None, :]
            sin = jnp.sin(freqs)[:, :, None, :]
            t1, t2 = (t[..., :D // 2], t[..., D // 2:])
            return jnp.concatenate([t1 * cos - t2 * sin, t2 * cos + t1 * sin], axis=-1)
        key = jax.random.key(seed)
        ks = jax.random.split(key, 10)
        x = jax.random.normal(ks[0], (B, S, HID), jnp.float32)
        Wq = jax.random.normal(ks[1], (HQ * D, HID), jnp.float32) * 0.02
        Wk = jax.random.normal(ks[2], (HK * D, HID), jnp.float32) * 0.02
        Wv = jax.random.normal(ks[3], (HK * D, HID), jnp.float32) * 0.02
        Wo = jax.random.normal(ks[4], (HID, HQ * D), jnp.float32) * 0.02
        q_norm_w = jax.random.uniform(ks[5], (D,), jnp.float32)
        k_norm_w = jax.random.uniform(ks[6], (D,), jnp.float32)
        k_cache = jax.random.normal(ks[7], (PAGES, PSIZE, HK, D), jnp.float32)
        v_cache = jax.random.normal(ks[8], (PAGES, PSIZE, HK, D), jnp.float32)
        block_table = jnp.arange(B * NPP, dtype=jnp.int32).reshape(B, NPP)
        cache_seqlens = jax.random.randint(ks[9], (B,), 0, 475).astype(jnp.int32)
        return dict(x=x, Wq=Wq, Wk=Wk, Wv=Wv, Wo=Wo, q_norm_w=q_norm_w, k_norm_w=k_norm_w, k_cache=k_cache, v_cache=v_cache, block_table=block_table, cache_seqlens=cache_seqlens)
    _L0_cond_all = _L0_cond_setup()
    _L0_cond_in = {k: v for k, v in _L0_cond_all.items() if k in ('Wq', 'Wk', 'Wv', 'Wo', 'q_norm_w', 'k_norm_w', 'k_cache', 'v_cache')}
    del _L0_cond_all

    def _L1_cond_setup():
        import jax, jax.numpy as jnp
        import numpy as np
        LORA_SCALING = 16.0 / 32.0
        key = jax.random.key(seed)
        k1, k2, k3, k4, k5 = jax.random.split(key, 5)
        B, S, D, R, L = (4, 256, 512, 32, 5)
        x = jax.random.normal(k1, (B, S, D), dtype=jnp.float32)
        weight = jax.random.normal(k2, (D, D), dtype=jnp.float32) * 0.02
        lora_A = jax.random.normal(k3, (L, D, R), dtype=jnp.float32) * 0.02
        lora_B_w = jax.random.normal(k4, (D, R), dtype=jnp.float32) * 0.02
        labeler_index = jax.random.randint(k5, (B,), 0, L, dtype=jnp.int32)
        return {'x': x, 'weight': weight, 'lora_A': lora_A, 'lora_B_w': lora_B_w, 'labeler_index': labeler_index}
    _L1_cond_all = _L1_cond_setup()
    _L1_cond_in = {k: v for k, v in _L1_cond_all.items() if k in ('weight', 'lora_A', 'lora_B_w')}
    del _L1_cond_all

    def _L2_cond_setup():
        import jax, jax.numpy as jnp
        import numpy as np
        TOP_K = 2
        LANG_BIAS = 5.0
        SCALING = 32.0 / 16.0
        LANGUAGE_PAD_ID = -1
        key = jax.random.key(seed)
        ks = jax.random.split(key, 6)
        B, T, D, O, E, R = (4, 256, 512, 512, 8, 16)
        x = jax.random.normal(ks[0], (B, T, D), dtype=jnp.float32)
        language_ids = jax.random.randint(ks[1], (B,), 0, E).astype(jnp.int64)
        W = jax.random.normal(ks[2], (O, D), dtype=jnp.float32) * (1.0 / np.sqrt(D))
        Wr = jax.random.normal(ks[3], (E, D), dtype=jnp.float32) * (1.0 / np.sqrt(D))
        A = jax.random.normal(ks[4], (E, R, D), dtype=jnp.float32) * (1.0 / np.sqrt(D))
        Bm = jax.random.normal(ks[5], (O, R), dtype=jnp.float32) * 0.0
        Bm = jnp.broadcast_to(Bm, (E, O, R)) + jax.random.normal(ks[5], (E, O, R), dtype=jnp.float32) * 0.02
        return {'x': x, 'language_ids': language_ids, 'W': W, 'Wr': Wr, 'A': A, 'B': Bm}
    _L2_cond_all = _L2_cond_setup()
    _L2_cond_in = {k: v for k, v in _L2_cond_all.items() if k in ('W', 'Wr', 'A', 'B')}
    del _L2_cond_all

    def _L3_cond_setup():
        import jax, jax.numpy as jnp
        import numpy as np
        B, N, H, F = (4, 64, 512, 1376)
        L, R, RANK = (1, 16, 16)
        SCALE = 0.5
        key = jax.random.key(seed)
        ks = jax.random.split(key, 12)
        nrm = lambda k, shape, fan: jax.random.normal(k, shape, jnp.float32) * fan ** (-0.5)
        inp = {'x': jax.random.normal(ks[0], (B, N, H), jnp.float32), 'W_gate': nrm(ks[1], (F, H), H), 'W_up': nrm(ks[2], (F, H), H), 'W_down': nrm(ks[3], (H, F), F), 'A_gate': nrm(ks[4], (L, R, RANK, H), H), 'B_gate': nrm(ks[5], (L, R, F, RANK), RANK), 'A_up': nrm(ks[6], (L, R, RANK, H), H), 'B_up': nrm(ks[7], (L, R, F, RANK), RANK), 'A_down': nrm(ks[8], (L, R, RANK, F), F), 'B_down': nrm(ks[9], (L, R, H, RANK), RANK), 'lora_indices': jax.random.randint(ks[10], (B,), 0, R), 'layer_idx': 0}
        return inp
    _L3_cond_all = _L3_cond_setup()
    _L3_cond_in = {k: v for k, v in _L3_cond_all.items() if k in ('W_gate', 'W_up', 'W_down', 'A_gate', 'B_gate', 'A_up', 'B_up', 'A_down', 'B_down')}
    del _L3_cond_all
    return {'x': x, 'itok_Bx16_0_63': itok_Bx16_0_63, 'itok_B_207_1644': itok_B_207_1644, 'itok_B_0_4': itok_B_0_4, 'itok_B_0_7': itok_B_0_7, 'itok_B_2_6': itok_B_2_6, 'L0_cond_Wq': _L0_cond_in['Wq'], 'L0_cond_Wk': _L0_cond_in['Wk'], 'L0_cond_Wv': _L0_cond_in['Wv'], 'L0_cond_Wo': _L0_cond_in['Wo'], 'L0_cond_q_norm_w': _L0_cond_in['q_norm_w'], 'L0_cond_k_norm_w': _L0_cond_in['k_norm_w'], 'L0_cond_k_cache': _L0_cond_in['k_cache'], 'L0_cond_v_cache': _L0_cond_in['v_cache'], 'L1_cond_weight': _L1_cond_in['weight'], 'L1_cond_lora_A': _L1_cond_in['lora_A'], 'L1_cond_lora_B_w': _L1_cond_in['lora_B_w'], 'L2_cond_W': _L2_cond_in['W'], 'L2_cond_Wr': _L2_cond_in['Wr'], 'L2_cond_A': _L2_cond_in['A'], 'L2_cond_B': _L2_cond_in['B'], 'L3_cond_W_gate': _L3_cond_in['W_gate'], 'L3_cond_W_up': _L3_cond_in['W_up'], 'L3_cond_W_down': _L3_cond_in['W_down'], 'L3_cond_A_gate': _L3_cond_in['A_gate'], 'L3_cond_B_gate': _L3_cond_in['B_gate'], 'L3_cond_A_up': _L3_cond_in['A_up'], 'L3_cond_B_up': _L3_cond_in['B_up'], 'L3_cond_A_down': _L3_cond_in['A_down'], 'L3_cond_B_down': _L3_cond_in['B_down']}

def reference(x, itok_Bx16_0_63, itok_B_207_1644, itok_B_0_4, itok_B_0_7, itok_B_2_6, L0_cond_Wq, L0_cond_Wk, L0_cond_Wv, L0_cond_Wo, L0_cond_q_norm_w, L0_cond_k_norm_w, L0_cond_k_cache, L0_cond_v_cache, L1_cond_weight, L1_cond_lora_A, L1_cond_lora_B_w, L2_cond_W, L2_cond_Wr, L2_cond_A, L2_cond_B, L3_cond_W_gate, L3_cond_W_up, L3_cond_W_down, L3_cond_A_gate, L3_cond_B_gate, L3_cond_A_up, L3_cond_B_up, L3_cond_A_down, L3_cond_B_down):
    import jax
    import jax.numpy as jnp

    def _L0_cond_ref(x, Wq, Wk, Wv, Wo, q_norm_w, k_norm_w, k_cache, v_cache, block_table, cache_seqlens):
        import jax, jax.numpy as jnp
        import numpy as np
        B, S, HID = (4, 128, 512)
        D, HQ, HK = (128, 32, 8)
        PAGES, PSIZE, NPP = (64, 32, 16)
        THETA = 10000.0
        EPS = 1e-06
        SCALE = 1.0 / float(np.sqrt(D))

        def _rmsnorm(t, w):
            var = jnp.mean(t * t, axis=-1, keepdims=True)
            return t * jax.lax.rsqrt(var + EPS) * w

        def _rope(t, pos):
            inv_freq = 1.0 / THETA ** (jnp.arange(0, D, 2, dtype=jnp.float32) / D)
            freqs = pos[..., None].astype(jnp.float32) * inv_freq
            cos = jnp.cos(freqs)[:, :, None, :]
            sin = jnp.sin(freqs)[:, :, None, :]
            t1, t2 = (t[..., :D // 2], t[..., D // 2:])
            return jnp.concatenate([t1 * cos - t2 * sin, t2 * cos + t1 * sin], axis=-1)
        bsz, seqlen, _ = x.shape
        q = jnp.einsum('bsd,ed->bse', x, Wq).reshape(bsz, seqlen, HQ, D)
        k = jnp.einsum('bsd,ed->bse', x, Wk).reshape(bsz, seqlen, HK, D)
        v = jnp.einsum('bsd,ed->bse', x, Wv).reshape(bsz, seqlen, HK, D)
        q = _rmsnorm(q, q_norm_w)
        k = _rmsnorm(k, k_norm_w)
        pos = cache_seqlens[:, None] + jnp.arange(seqlen)[None, :]
        q = _rope(q, pos)
        k = _rope(k, pos)
        L = NPP * PSIZE
        kc = k_cache[block_table].reshape(bsz, L, HK, D)
        vc = v_cache[block_table].reshape(bsz, L, HK, D)
        k_all = jnp.concatenate([kc, k], axis=1)
        v_all = jnp.concatenate([vc, v], axis=1)
        valid_c = jnp.arange(L)[None, :] < cache_seqlens[:, None]
        valid = jnp.concatenate([valid_c, jnp.ones((bsz, seqlen), dtype=bool)], axis=1)
        rep = HQ // HK
        k_all = jnp.repeat(k_all, rep, axis=2)
        v_all = jnp.repeat(v_all, rep, axis=2)
        scores = jnp.einsum('bqhd,bkhd->bhqk', q, k_all) * SCALE
        scores = jnp.where(valid[:, None, None, :], scores, -1e+30)
        probs = jax.nn.softmax(scores, axis=-1)
        o = jnp.einsum('bhqk,bkhd->bqhd', probs, v_all)
        o = o.reshape(bsz, seqlen, HQ * D)
        return jnp.einsum('bse,de->bsd', o, Wo)

    def _L1_cond_ref(x, weight, lora_A, lora_B_w, labeler_index):
        import jax, jax.numpy as jnp
        import numpy as np
        LORA_SCALING = 16.0 / 32.0
        result = jnp.einsum('bsd,od->bso', x, weight)
        labelers_A = lora_A[labeler_index]
        low = jnp.einsum('bsd,bdr->bsr', x, labelers_A)
        result = result + jnp.einsum('bsr,or->bso', low, lora_B_w) * LORA_SCALING
        return result

    def _L2_cond_ref(x, language_ids, W, Wr, A, B):
        import jax, jax.numpy as jnp
        import numpy as np
        TOP_K = 2
        LANG_BIAS = 5.0
        SCALING = 32.0 / 16.0
        LANGUAGE_PAD_ID = -1
        base = jnp.einsum('btd,od->bto', x, W)
        E = Wr.shape[0]
        logits = jnp.einsum('btd,ed->bte', x.astype(jnp.float32), Wr.astype(jnp.float32))
        expert_targets = language_ids
        valid = expert_targets >= 0
        tgt = jnp.where(valid, expert_targets, 0)
        bias = jax.nn.one_hot(tgt, E, dtype=logits.dtype) * LANG_BIAS
        bias = jnp.where(valid[:, None], bias, 0.0)
        logits = logits + bias[:, None, :]
        topw, topi = jax.lax.top_k(logits, TOP_K)
        weights = jax.nn.softmax(topw, axis=-1)
        gates = jnp.sum(jax.nn.one_hot(topi, E, dtype=weights.dtype) * weights[..., None], axis=-2)
        gates = gates.astype(x.dtype)
        h = jnp.einsum('btd,erd->bter', x, A)
        lora_out = jnp.einsum('bter,bte,eor->bto', h, gates, B)
        return base + SCALING * lora_out

    def _L3_cond_ref(x, W_gate, W_up, W_down, A_gate, B_gate, A_up, B_up, A_down, B_down, lora_indices, layer_idx):
        import jax, jax.numpy as jnp
        import numpy as np
        B, N, H, F = (4, 64, 512, 1376)
        L, R, RANK = (1, 16, 16)
        SCALE = 0.5

        def lora_add(base, inp, A, B):
            Ab = A[layer_idx][lora_indices]
            Bb = B[layer_idx][lora_indices]
            t = jnp.einsum('bri,bni->bnr', Ab, inp)
            return base + jnp.einsum('bor,bnr->bno', Bb, t) * SCALE
        gate = lora_add(jnp.einsum('bnh,fh->bnf', x, W_gate), x, A_gate, B_gate)
        up = lora_add(jnp.einsum('bnh,fh->bnf', x, W_up), x, A_up, B_up)
        act = jax.nn.silu(gate) * up
        down = lora_add(jnp.einsum('bnf,hf->bnh', act, W_down), act, A_down, B_down)
        return down
    x = x + _L0_cond_ref(x, L0_cond_Wq, L0_cond_Wk, L0_cond_Wv, L0_cond_Wo, L0_cond_q_norm_w, L0_cond_k_norm_w, L0_cond_k_cache, L0_cond_v_cache, itok_Bx16_0_63, itok_B_207_1644)
    x = x + _L1_cond_ref(x, L1_cond_weight, L1_cond_lora_A, L1_cond_lora_B_w, itok_B_0_4)
    x = x + _L2_cond_ref(x, itok_B_0_7, L2_cond_W, L2_cond_Wr, L2_cond_A, L2_cond_B)
    x = x + _L3_cond_ref(x, L3_cond_W_gate, L3_cond_W_up, L3_cond_W_down, L3_cond_A_gate, L3_cond_B_gate, L3_cond_A_up, L3_cond_B_up, L3_cond_A_down, L3_cond_B_down, itok_B_2_6, 0)
    return x

_drawn_inputs = setup_inputs


def setup_inputs(seed=0):
    import zlib

    import numpy as np

    out = dict(_drawn_inputs(seed))
    spreads = {}
    factors = {'L0_cond_Wk': 8.0,
     'L0_cond_Wv': 12.771,
     'L0_cond_k_norm_w': 8.0,
     'L2_cond_Wr': 2.934,
     'L0_cond_k_cache': 7.633,
     'L0_cond_v_cache': 4.516}
    for name, (base, spread) in spreads.items():
        noise = np.random.default_rng([zlib.crc32(name.encode()), seed]).standard_normal(out[name].shape)
        drawn = base * np.exp(spread * noise) if base else spread * noise
        out[name] = jnp.asarray(drawn.astype(out[name].dtype))
    for name, factor in factors.items():
        out[name] = (out[name] * factor).astype(out[name].dtype)
    return out
```

```python
from contextlib import ExitStack

import numpy as np

import concourse.bass as bass
from concourse import mybir

F32 = mybir.dt.float32
F32R = mybir.dt.float32r
I32 = mybir.dt.int32
ALU = mybir.AluOpType
ACT = mybir.ActivationFunctionType

P = 128
B, S, HID = 8, 128, 512
D, HQ, HK = 128, 32, 8
REP = HQ // HK
PAGES, PSIZE, NPP = 64, 32, 16
CACHE = NPP * PSIZE
KEYS = CACHE + S
KC = KEYS // P
HALF = KEYS // 2
DC = HID // P
NT = HK * B
GW = (REP * DC + 2 * DC + REP * DC) * P
PIECES = 8
PW = GW // PIECES
WKV = REP * DC * P
WWO = WKV + 2 * DC * P
QKV_PIECES = -(-WWO // PW)
POS_END = 1645
EPS = 1e-6
NEG = -1e30

R1 = 32
LORA1_SCALE = 0.5
E, R2 = 8, 16
LANG_BIAS, LORA2_SCALE = 5.0, 2.0
ER = E * R2
F, R3 = 1376, 16
BR = B * R3
LORA3_SCALE = 0.5
FT = -(-F // P)
FP = FT * P
HB = B // 2
HT = HB * S
FW = (DC + 1) * P * 2 + HID + P
F_GATE, F_GATE_B, F_UP, F_UP_B, F_DOWN, F_DOWN_A = 0, 512, 640, 1152, 1280, 1792


def ds(i, n=1):
    return bass.ds(i, n)


def build(nc, t, out):
    ctx = ExitStack()
    with ctx:
        def sb(name, shape, dt=F32, where=ctx):
            return where.enter_context(nc.sbuf_tensor(name, shape, dt))

        def sem(name):
            return ctx.enter_context(nc.semaphore(name))

        ident = sb("ident", [P, P])
        spare = sb("spare", [P, 16])
        acc = sb("acc", [P, B, HID])

        banks = ctx.enter_context(nc.psum_tensor("banks", [P, 8, 512], F32))
        score_ps = [banks[:, 0:2, :], banks[:, 2:4, :]]
        pt_ps = banks[:, 4:6, :].rearrange("p a n -> p (a n)")[:, 0:KEYS]
        q_ps = banks[:, 6, :]
        misc_ps = banks[:, 7, :]
        kt_ps = banks[:, 0:2, :].rearrange("p a n -> p (a n)")[:, 0:KEYS]

        att = ExitStack()
        tabs = sb("tabs", [P, B, 4, P], where=att)
        iota = sb("iota", [P, CACHE], where=att)
        mask = sb("mask", [P, 2, KEYS], where=att)
        seq_i = sb("seq_i", [P, B], I32, where=att)
        seq_f = sb("seq_f", [P, B], where=att)
        half_neg = sb("half_neg", [P, REP], where=att)
        w_raw = sb("w_raw", [P, 2, PW], where=att)
        w_pair = sb("w_pair", [P, 2, 2 * GW], F32R, where=att)
        x_raw = sb("x_raw", [P, 2, DC * P], where=att)
        x_pair = [sb(f"x_pair{i}", [P, 2, DC, P], F32R, where=att) for i in range(2)]
        kv_raw = sb("kv_raw", [P, 2, KC, 2 * D], where=att)
        v_pair = [sb(f"v_pair{i}", [P, 2, KC, D], F32R, where=att) for i in range(2)]
        kt_pair = sb("kt_pair", [P, 2, KEYS], F32R, where=att)
        qt_pair = sb("qt_pair", [P, 2, REP, P], F32R, where=att)
        pt_pair = sb("pt_pair", [P, 2, REP, KC, P], F32R, where=att)
        o_pair = sb("o_pair", [P, 2, REP, P], F32R, where=att)
        prob = sb("prob", [P, REP, KEYS], where=att)
        q_sb = sb("q_sb", [P, REP, P], where=att)
        q_cos = sb("q_cos", [P, REP, P], where=att)
        q_sin = sb("q_sin", [P, REP, P], where=att)
        k_cos = sb("k_cos", [P, P], where=att)
        k_sin = sb("k_sin", [P, P], where=att)
        squares = sb("squares", [P, P], where=att)
        q_ss = sb("q_ss", [P, REP], where=att)
        q_se = sb("q_se", [P, REP], where=att)
        q_rs = [sb(f"q_rs{i}", [P, REP], where=att) for i in range(2)]
        k_ss = sb("k_ss", [P, 1], where=att)
        k_se = sb("k_se", [P, 1], where=att)
        k_rs = sb("k_rs", [P, 1], where=att)
        smax = sb("smax", [P, REP], where=att)
        nbias = sb("nbias", [P, REP], where=att)
        psum_row = sb("psum_row", [P, REP], where=att)
        rsum = sb("rsum", [P, REP], where=att)
        trig = prob[:, 0:2, :].rearrange("p a n -> p (a n)")[:, 0:B * D].rearrange("p (b d) -> p b d", b=B)
        wnorm = prob[:, 2, 0:2 * D].rearrange("p (a d) -> p a d", a=2)

        att.close()

        fw_raw = [sb(f"fw_raw{i}", [P, FW]) for i in range(2)]
        fw_pair = [sb(f"fw_pair{i}", [P, 2, FW], F32R) for i in range(2)]
        gu_b = sb("gu_b", [P, 2, FP])
        d_a = sb("d_a", [P, FT, BR])
        gu_a = sb("gu_a", [P, 2, B, DC * R3])
        d_b = sb("d_b", [P, HID])
        x3t_pair = sb("x3t_pair", [P, 2, DC, B * S], F32R)
        own_rows = sb("own_rows", [P, B])
        mix = ExitStack()
        w12_raw = sb("w12_raw", [P, DC * HID], where=mix)
        w1_pair = sb("w1_pair", [P, 2, DC, HID], F32R, where=mix)
        w2_pair = sb("w2_pair", [P, 2, DC, HID], F32R, where=mix)
        a1_raw = sb("a1_raw", [P, B, DC, R1], where=mix)
        a1_pair = sb("a1_pair", [P, 2, DC, P], F32R, where=mix)
        b1_raw = sb("b1_raw", [R1, HID], where=mix)
        b1_pair = sb("b1_pair", [R1, 2, HID], F32R, where=mix)
        ra_raw = sb("ra_raw", [P, DC, E + ER], where=mix)
        ra_pair = sb("ra_pair", [P, 2, DC, E + ER], F32R, where=mix)
        b2_raw = sb("b2_raw", [P, HID], where=mix)
        b2_pair = sb("b2_pair", [P, 2, HID], F32R, where=mix)
        x1_sb = sb("x1_sb", [P, HID], where=mix)
        x2_sb = sb("x2_sb", [P, HID], where=mix)
        x3_sb = sb("x3_sb", [P, HID], where=mix)
        x1t_pair = sb("x1t_pair", [P, 2, DC, P], F32R, where=mix)
        x2t_pair = sb("x2t_pair", [P, 2, DC, P], F32R, where=mix)
        low_pair = sb("low_pair", [R1, 2, P], F32R, where=mix)
        hg = sb("hg", [P, E, R2], where=mix)
        hgt_pair = sb("hgt_pair", [P, 2, P], F32R, where=mix)
        lang_i = sb("lang_i", [P, B], I32, where=mix)
        lang_f = sb("lang_f", [P, B], where=mix)
        experts = sb("experts", [P, E], where=mix)
        lower = sb("lower", [P, E, E], where=mix)
        lbias = sb("lbias", [P, B, E], where=mix)
        logits = sb("logits", [P, E], where=mix)
        top = sb("top", [P, 1], where=mix)
        above = sb("above", [P, E, E], where=mix)
        equal = sb("equal", [P, E, E], where=mix)
        rank = sb("rank", [P, E], where=mix)
        expl = sb("expl", [P, E], where=mix)
        gate = sb("gate", [P, E], where=mix)
        gsum = sb("gsum", [P, 1], where=mix)
        grec = sb("grec", [P, 1], where=mix)
        mix.close()
        ga_f = sb("ga_f", [P, 2, DC, BR])
        ga_pair = [sb(f"ga_pair{i}", [P, 2, DC, BR], F32R) for i in range(2)]
        db_pair = sb("db_pair", [P, 2, HID], F32R)
        own_f = sb("own_f", [P, HB, S])
        tg_pair = [sb(f"tg_pair{i}", [P, 2, HT], F32R) for i in range(2)]
        td_pair = sb("td_pair", [P, 2, HT], F32R)
        sig = sb("sig", [P, HT])
        gsig = sb("gsig", [P, HT])
        act_f = sb("act_f", [P, HT])
        act_pair = [sb(f"act_pair{i}", [P, 2, HT], F32R) for i in range(2)]
        ffn_bank = [banks[:, j, :] for j in range(HB)]
        t_ps, g_ps, u_ps = banks[:, 4, :], banks[:, 5, :], banks[:, 6, :]

        s_const = sem("s_const")
        s_trig = sem("s_trig")
        s_acc0 = sem("s_acc0")
        s_xin = [sem(f"s_xin{i}") for i in range(2)]
        s_win = [sem(f"s_win{i}") for i in range(2)]
        s_kvin = [sem(f"s_kvin{i}") for i in range(2)]
        x_hi, x_lo = sem("x_hi"), sem("x_lo")
        w_hi, w_lo = sem("w_hi"), sem("w_lo")
        v_hi, v_lo = sem("v_hi"), sem("v_lo")
        tab_done = sem("tab_done")
        halves = sem("halves")
        seq_done = sem("seq_done")
        mask_done = sem("mask_done")
        q_done = sem("q_done")
        q_copied = sem("q_copied")
        q_sq = sem("q_sq")
        q_eps = sem("q_eps")
        q_rsd = sem("q_rsd")
        q_mul = sem("q_mul")
        q_rot = sem("q_rot")
        qt_done = sem("qt_done")
        qt_hi, qt_lo = sem("qt_hi"), sem("qt_lo")
        kvp_done = sem("kvp_done")
        kv_copied = sem("kv_copied")
        k_sq = sem("k_sq")
        k_eps = sem("k_eps")
        k_rsd = sem("k_rsd")
        k_mul = sem("k_mul")
        k_rot = sem("k_rot")
        kt_done = sem("kt_done")
        kt_hi, kt_lo = sem("kt_hi"), sem("kt_lo")
        scored = sem("scored")
        masked = sem("masked")
        biased = sem("biased")
        exped = sem("exped")
        recip = sem("recip")
        normed = sem("normed")
        t_done = sem("t_done")
        pt_hi, pt_lo = sem("pt_hi"), sem("pt_lo")
        pv_done = sem("pv_done")
        o_hi, o_lo = sem("o_hi"), sem("o_lo")
        wo_done = sem("wo_done")
        added = sem("added")
        stored = sem("stored")
        s_w1, s_w2, s_a1, s_small = sem("s_w1"), sem("s_w2"), sem("s_a1"), sem("s_small")
        s_ffs = sem("s_ffs")
        w12_hi, w12_lo = sem("w12_hi"), sem("w12_lo")
        sm_hi, sm_lo = sem("sm_hi"), sem("sm_lo")
        a1_zero, a1_hi, a1_lo = sem("a1_zero"), sem("a1_hi"), sem("a1_lo")
        lang_done, lbias_done = sem("lang_done"), sem("lbias_done")
        x1_done, x1t_done, x1t_hi, x1t_lo = sem("x1_done"), sem("x1t_done"), sem("x1t_hi"), sem("x1t_lo")
        low_done, low_hi, low_lo = sem("low_done"), sem("low_hi"), sem("low_lo")
        y1_done = sem("y1_done")
        x2_done, x2t_done, x2t_hi, x2t_lo = sem("x2_done"), sem("x2t_done"), sem("x2t_hi"), sem("x2t_lo")
        hl_done = sem("hl_done")
        gates = sem("gates")
        exp_done = sem("exp_done")
        hgt_done, hgt_hi, hgt_lo = sem("hgt_done"), sem("hgt_hi"), sem("hgt_lo")
        y2_done = sem("y2_done")
        top_done, x3_kept = sem("top_done"), sem("x3_kept")
        GSTEPS = 11
        x3_done, x3t_done, x3t_hi, x3t_lo = sem("x3_done"), sem("x3t_done"), sem("x3t_hi"), sem("x3t_lo")
        s_fw = [sem(f"s_fw{i}") for i in range(2)]
        s_fwx = [sem(f"s_fwx{i}") for i in range(2)]
        fw_hi, fw_lo = sem("fw_hi"), sem("fw_lo")
        ga_got, ga_hi, ga_lo = sem("ga_got"), sem("ga_hi"), sem("ga_lo")
        db_hi, db_lo = sem("db_hi"), sem("db_lo")
        tg_done, tg_own, tg_hi, tg_lo = sem("tg_done"), sem("tg_own"), sem("tg_hi"), sem("tg_lo")
        g_done, u_done = sem("g_done"), sem("u_done")
        sig_done, gsig_done, act_done = sem("sig_done"), sem("gsig_done"), sem("act_done")
        act_hi, act_lo = sem("act_hi"), sem("act_lo")
        down_done = sem("down_done")
        td_own, td_hi, td_lo = sem("td_own"), sem("td_hi"), sem("td_lo")
        ffn_done, ffn_added = sem("ffn_done"), sem("ffn_added")

        block = ctx.enter_context(nc.Block())

        def product(e, dst, lhs, rhs, first, last):
            e.matmul(dst, lhs(0), rhs(0), start=first, stop=False)
            e.matmul(dst, lhs(0), rhs(1), start=False, stop=False)
            return e.matmul(dst, lhs(1), rhs(0), start=False, stop=last)

        def steps(e, step):
            step(0, 0)
            with e.Fori(0, (NT - PIECES - 2) // 2) as i:
                step(2 * i + 1, 1)
                step(2 * i + 2, 0)
            step(NT - PIECES - 1, 1)
            with e.Fori(0, (PIECES - 2) // 2) as i:
                step(2 * i + NT - PIECES, 0, w=False)
                step(2 * i + NT - PIECES + 1, 1, w=False)
            step(NT - 2, 0, x=False, w=False)
            step(NT - 1, 1, x=False, w=False, nxt=False)

        def tiles(e, half, step):
            odd = (half * FT) % 2
            step(1, 1 - odd)
            step(2, odd)
            with e.Fori(0, (FT - 3) // 2) as i:
                step(2 * i + 3, 1 - odd)
                step(2 * i + 4, odd)

        def settle(e, k):
            e.tensor_tensor(spare[:, k:k + 1], ident[:, 0:1], ident[:, 0:1], ALU.mult)

        @block.sync
        def _(sp):
            def load_x(n, par):
                sp.dma_start(x_raw[:, par, :], t["xT"][ds(n % B), :, :].rearrange("a p n -> p (a n)")).then_inc(s_xin[par], 16)

            def load_w(m, par):
                sp.dma_start(w_raw[:, par, :], t["w_att"][ds(m), :, :].rearrange("a p n -> p (a n)")).then_inc(s_win[par], 16)

            def load_kv(n, par, used=False):
                g, b = n // B, n % B
                _, pages = nc.values_load_multi_w_load_instructions(
                    t["pages"][ds(b), :], engines=[sp.engine], min_val=0, max_val=PAGES - 1,
                    skip_runtime_bounds_check_because="page numbers are below PAGES")
                if used:
                    sp.wait_ge(v_lo, n - 1)
                    sp.wait_ge(kt_done, n - 1)
                for j, page in enumerate(pages):
                    a = PSIZE * (j % 4)
                    sp.dma_start(kv_raw[a:a + PSIZE, par, j // 4, :],
                                 t["kv"][ds(g), ds(page), :, :].rearrange("g a s n -> s (g a n)")).then_inc(s_kvin[par], 16)

            sp.dma_start(ident[:], t["ident"]).then_inc(s_const, 16)
            sp.dma_start(iota[:], t["iota"].partition_broadcast(P)).then_inc(s_const, 16)
            sp.dma_start(seq_i[:], t["seqlens"].partition_broadcast(P)).then_inc(s_const, 16)
            load_x(0, 0)
            load_w(0, 0)
            _, lengths = nc.values_load_multi_w_load_instructions(
                t["seqlens"].unsqueeze(0), engines=[sp.engine], min_val=0, max_val=POS_END - 1,
                skip_runtime_bounds_check_because="cache lengths are below POS_END")
            for b in range(B):
                sp.dma_start(trig[:, b, :], t["trig"][ds(lengths[b], S), :]).then_inc(s_trig, 16)
            sp.dma_start(wnorm, t["wnorm"].partition_broadcast(P)).then_inc(s_trig, 16)
            load_w(1, 1)
            load_x(1, 1)
            load_kv(0, 0)
            for m in range(2, PIECES):
                sp.wait_ge(w_lo, m - 1)
                load_w(m, m % 2)
            sp.dma_start(acc[:], t["x"].rearrange("b s n -> s b n")).then_inc(s_acc0, 16)
            load_kv(1, 1)
            sp.wait_ge(x_lo, 1)
            load_x(2, 0)
            sp.wait_ge(w_lo, PIECES - 1)
            load_w(PIECES, 0)

            def step(n, par, x=True, w=True):
                if w:
                    sp.wait_ge(w_lo, n + PIECES)
                    load_w(n + 1 + PIECES, 1 - par)
                if x:
                    sp.wait_ge(x_lo, n + 2)
                    load_x(n + 3, 1 - par)
                load_kv(n + 2, par, True)

            last_w = NT - PIECES - 1
            step(0, 0)
            with sp.Fori(0, (last_w - 1) // 2) as i:
                step(2 * i + 1, 1)
                step(2 * i + 2, 0)
            for n in range(last_w, NT - 2):
                step(n, n % 2, x=n + 3 < NT, w=False)

            sp.wait_ge(added, NT)
            sp.dma_start(w12_raw[:], t["w12"][0]).then_inc(s_w1, 16)
            _, labels = nc.values_load_multi_w_load_instructions(
                t["label"].unsqueeze(0), engines=[sp.engine], min_val=0, max_val=4,
                skip_runtime_bounds_check_because="indices of block 1's LoRA are below 5")
            for b in range(B):
                sp.dma_start(a1_raw[:, b].rearrange("p c r -> p (c r)"),
                             t["a1"][ds(labels[b]), :, :].rearrange("a p n -> p (a n)")).then_inc(s_a1, 16)
            sp.dma_start(b1_raw[:], t["b1"]).then_inc(s_small, 16)
            sp.dma_start(ra_raw[:].rearrange("p c n -> p (c n)"), t["ra"]).then_inc(s_small, 16)
            sp.dma_start(b2_raw[:], t["b2"]).then_inc(s_small, 16)
            sp.dma_start(lang_i[:], t["lang"].partition_broadcast(P)).then_inc(s_small, 16)
            sp.dma_start(experts[:], t["experts"].partition_broadcast(P)).then_inc(s_small, 16)
            sp.dma_start(lower[:].rearrange("p a b -> p (a b)"), t["lower"].partition_broadcast(P)).then_inc(s_small, 16)
            sp.dma_start(own_rows[:], t["own"]).then_inc(s_small, 16)
            sp.wait_ge(w12_lo, 1)
            sp.dma_start(w12_raw[:], t["w12"][1]).then_inc(s_w2, 16)
            _, loras = nc.values_load_multi_w_load_instructions(
                t["lora"].unsqueeze(0), engines=[sp.engine], min_val=0, max_val=15,
                skip_runtime_bounds_check_because="indices of the feed-forward's LoRA are below 16")
            for b in range(B):
                rows = slice(b * R3, (b + 1) * R3)
                for k in range(2):
                    sp.dma_start(gu_a[:, k, b, :], t["gu_a"][k, ds(loras[b]), :, :].rearrange("a p n -> p (a n)")).then_inc(s_ffs, 16)
                    sp.dma_start(gu_b[rows, k, :], t["gu_b"][k, ds(loras[b]), :, :].rearrange("a r n -> r (a n)")).then_inc(s_ffs, 16)
                sp.dma_start(d_a[:, :, rows], t["d_a"][ds(loras[b]), :, :, :].rearrange("a p f r -> p (a f) r")).then_inc(s_ffs, 16)
                sp.dma_start(d_b[rows, :], t["d_b"][ds(loras[b]), :, :].rearrange("a r n -> r (a n)")).then_inc(s_ffs, 16)
            sp.wait_ge(s_ffs, 16 * 6 * B)

            def load_fw(m, ft, par):
                raw = fw_raw[par]
                for lo, hi, src in ((F_GATE, F_GATE_B, 0), (F_UP, F_UP_B, 1), (F_DOWN, F_DOWN_A, 2)):
                    sp.dma_start(raw[:, lo:hi], t["fw"][src, ds(ft), :, :].rearrange("a p n -> p (a n)")).then_inc(s_fw[par], 16)
                for at, src in ((F_GATE_B, gu_b[:, 0, ds(ft * P, P)]), (F_UP_B, gu_b[:, 1, ds(ft * P, P)]),
                                (F_DOWN_A, d_a[:, ds(ft), :].rearrange("p f n -> p (f n)"))):
                    sp.dma_start(raw[:, at:at + P], src).then_inc(s_fwx[par], 16)

            load_fw(0, 0, 0)
            for half in range(2):
                if half:
                    sp.wait_ge(fw_lo, FT - 1)
                    load_fw(FT, 0, 1)

                def load_step(ft, par):
                    if not (half == 0 and isinstance(ft, int) and ft == 1):
                        sp.wait_ge(fw_lo, half * FT + ft - 1)
                    load_fw(half * FT + ft, ft, par)

                tiles(sp, half, load_step)
            for b in range(B):
                sp.wait_ge(ffn_added, b + 1)
                sp.dma_start(out[b], acc[:, b, :]).then_inc(stored, 16)
            sp.wait_ge(stored, 16 * B)

        @block.gpsimd
        def _(pool):
            def x_low(n, par):
                pool.wait_ge(x_hi, n + 1)
                pool.tensor_tensor(x_pair[par][:, 1], x_raw[:, par, :].rearrange("p (c n) -> p c n", c=DC),
                                   x_pair[par][:, 0].bitcast(F32), ALU.subtract).then_inc(x_lo, 1)

            def w_low(m, par):
                at = (m % (2 * PIECES)) * PW
                pool.wait_ge(w_hi, m + 1)
                pool.tensor_tensor(w_pair[:, 1, ds(at, PW)], w_raw[:, par, :],
                                   w_pair[:, 0, ds(at, PW)].bitcast(F32), ALU.subtract).then_inc(w_lo, 1)

            def v_low(n, par):
                pool.wait_ge(v_hi, n + 1)
                pool.tensor_tensor(v_pair[par][:, 1], kv_raw[:, par, :, D:2 * D],
                                   v_pair[par][:, 0].bitcast(F32), ALU.subtract).then_inc(v_lo, 1)

            def q_norm(n, par):
                pool.wait_ge(q_sq, n + 1)
                settle(pool, 0)
                pool.tensor_scalar(q_se[:], q_ss[:], D * EPS, None, ALU.add).then_inc(q_eps, 1)
                pool.wait_ge(q_eps, n + 1)
                pool.tensor_tensor(q_rs[par][:], q_se[:], half_neg[:], ALU.pow).then_inc(q_rsd, 1)

            def k_norm(n):
                pool.wait_ge(k_sq, n + 1)
                settle(pool, 1)
                pool.tensor_scalar(k_se[:], k_ss[:], D * EPS, None, ALU.add).then_inc(k_eps, 1)
                pool.wait_ge(k_eps, n + 1)
                pool.tensor_tensor(k_rs[:], k_se[:], half_neg[:, 0:1], ALU.pow).then_inc(k_rsd, 1)

            def q_rotate(n):
                pool.wait_ge(q_mul, 2 * n + 2)
                h = D // 2
                pool.tensor_tensor(q_cos[:, :, 0:h], q_cos[:, :, 0:h], q_sin[:, :, h:D], ALU.add)
                pool.tensor_tensor(q_cos[:, :, h:D], q_cos[:, :, h:D], q_sin[:, :, 0:h], ALU.add).then_inc(q_rot, 1)

            def k_rotate(n, par):
                pool.wait_ge(k_mul, 2 * n + 2)
                h = D // 2
                dst = kv_raw[:, par, KC - 1, 0:D]
                pool.tensor_tensor(dst[:, 0:h], k_cos[:, 0:h], k_sin[:, h:D], ALU.add)
                pool.tensor_tensor(dst[:, h:D], k_cos[:, h:D], k_sin[:, 0:h], ALU.add).then_inc(k_rot, 1)

            pool.memset(mask[:, :, CACHE:KEYS], 0.0)
            pool.memset(half_neg[:], -0.5).then_inc(halves, 1)
            x_low(0, 0)
            for m in range(QKV_PIECES):
                w_low(m, m % 2)
            pool.wait_ge(halves, 1)
            k_norm(0)
            k_rotate(0, 0)
            q_rotate(0)
            q_norm(0, 0)
            x_low(1, 1)
            for m in range(QKV_PIECES, PIECES):
                w_low(m, m % 2)

            def step(n, par, x=True, w=True, nxt=True):
                v_low(n, par)
                if w:
                    w_low(n + PIECES, par)
                if nxt:
                    k_norm(n + 1)
                    k_rotate(n + 1, 1 - par)
                    q_rotate(n + 1)
                    q_norm(n + 1, 1 - par)
                if x:
                    x_low(n + 2, par)

            steps(pool, step)

            pool.wait_ge(s_w1, 16)
            pool.memset(a1_pair[:].rearrange("p k c n -> p (k c n)").bitcast(F32), 0.0).then_inc(a1_zero, 1)

            def a1_low(b):
                pool.wait_ge(a1_hi, b + 1)
                pool.tensor_tensor(a1_pair[:, 1, :, 0:R1], a1_raw[:, ds(b), :, :].rearrange("p b c r -> p (b c) r"),
                                   a1_pair[:, 0, :, 0:R1].bitcast(F32), ALU.subtract).then_inc(a1_lo, 1)

            a1_low(0)
            with pool.Fori(1, B) as b:
                a1_low(b)

            def fw_low(m, par):
                pool.wait_ge(fw_hi, m + 1)
                pool.tensor_tensor(fw_pair[par][:, 1], fw_raw[par][:], fw_pair[par][:, 0].bitcast(F32),
                                   ALU.subtract).then_inc(fw_lo, 1)

            fw_low(0, 0)
            for half in range(2):
                if half:
                    fw_low(FT, 1)
                tiles(pool, half, lambda ft, par: fw_low(half * FT + ft, par))

        @block.scalar
        def _(act):
            def copy_q(n):
                act.wait_ge(q_done, n + 1)
                if not (isinstance(n, int) and n == 0):
                    act.wait_ge(q_mul, 2 * n)
                act.activation(q_sb[:].rearrange("p h d -> p (h d)"), q_ps, ACT.Copy).then_inc(q_copied, 1)
                act.wait_ge(q_copied, n + 1)
                for h in range(REP):
                    last = act.activation(q_ps[:, h * D:(h + 1) * D], q_sb[:, h, :], ACT.Square, accum_out=q_ss[:, h:h + 1])
                last.then_inc(q_sq, 1)

            def copy_kv(n, par):
                act.wait_ge(kvp_done, n + 1)
                if not (isinstance(n, int) and n < 2):
                    act.wait_ge(v_lo, n - 1)
                    act.wait_ge(kt_done, n - 1)
                act.activation(kv_raw[:, par, KC - 1, :], misc_ps[:, 0:2 * D], ACT.Copy).then_inc(kv_copied, 1)
                act.wait_ge(kv_copied, n + 1)
                act.activation(squares[:], kv_raw[:, par, KC - 1, 0:D], ACT.Square, accum_out=k_ss[:]).then_inc(k_sq, 1)

            def x_high(n, par):
                act.wait_ge(s_xin[par], 16 * (n // 2 + 1))
                if not (isinstance(n, int) and n < 2):
                    act.wait_ge(kvp_done, n - 1)
                act.activation(x_pair[par][:, 0], x_raw[:, par, :].rearrange("p (c n) -> p c n", c=DC),
                               ACT.Copy).then_inc(x_hi, 1)

            def v_high(n, par):
                act.wait_ge(s_kvin[par], 16 * NPP * (n // 2 + 1))
                if not (isinstance(n, int) and n < 2):
                    act.wait_ge(pv_done, n - 1)
                act.activation(v_pair[par][:, 0], kv_raw[:, par, :, D:2 * D], ACT.Copy).then_inc(v_hi, 1)

            def qt_high(n):
                act.wait_ge(qt_done, n + 1)
                act.activation(qt_pair[:, 0].rearrange("p h n -> p (h n)"), q_ps, ACT.Copy).then_inc(qt_hi, 1)

            def kt_high(n):
                act.wait_ge(kt_done, n + 1)
                act.activation(kt_pair[:, 0], kt_ps, ACT.Copy).then_inc(kt_hi, 1)

            def o_high(n):
                act.wait_ge(pv_done, n + 1)
                act.activation(o_pair[:, 0].rearrange("p h n -> p (h n)"), misc_ps, ACT.Copy).then_inc(o_hi, 1)

            def pt_high(n, h):
                act.wait_ge(t_done, REP * n + h + 1)
                act.activation(pt_pair[:, 0, h].rearrange("p c n -> p (c n)"), pt_ps, ACT.Copy).then_inc(pt_hi, 1)

            def exponent(n, par, h):
                act.wait_ge(biased, REP * n + h + 1)
                act.wait_ge(q_rsd, n + 1)
                act.activation(prob[:, h, :], prob[:, h, :], ACT.Exp, bias=nbias[:, h:h + 1],
                               scale=q_rs[par][:, h:h + 1], accum_out=psum_row[:, h:h + 1]).then_inc(exped, 1)

            def step(n, par, x=True, w=True, nxt=True):
                first = isinstance(n, int) and n == 0
                exponent(n, par, 0)
                exponent(n, par, 1)
                v_high(n, par)
                if not first:
                    o_high(n - 1)
                pt_high(n, 0)
                exponent(n, par, 2)
                if nxt:
                    copy_kv(n + 1, 1 - par)
                if x:
                    x_high(n + 2, par)
                pt_high(n, 1)
                if nxt:
                    copy_q(n + 1)
                    kt_high(n + 1)
                pt_high(n, 2)
                exponent(n, par, 3)
                if nxt:
                    qt_high(n + 1)
                pt_high(n, 3)

            x_high(0, 0)
            copy_kv(0, 0)
            copy_q(0)
            x_high(1, 1)
            kt_high(0)
            qt_high(0)
            steps(act, step)
            o_high(NT - 1)

            def to_high(dst, src, done, count, hi_sem, scale=1.0):
                act.wait_ge(done, count)
                act.activation(dst, src, ACT.Copy, scale=scale).then_inc(hi_sem, 1)

            to_high(w1_pair[:, 0].rearrange("p c n -> p (c n)"), w12_raw[:], s_w1, 16, w12_hi)
            act.wait_ge(s_small, 16 * 7)
            act.activation(b1_pair[:, 0], b1_raw[:], ACT.Copy)
            act.activation(ra_pair[:, 0], ra_raw[:], ACT.Copy)
            act.activation(b2_pair[:, 0], b2_raw[:], ACT.Copy).then_inc(sm_hi, 1)

            def stage_a(b):
                to_high(x1t_pair[:, 0].rearrange("p c n -> p (c n)"), banks[:, 0, :], x1t_done, b + 1, x1t_hi)
                to_high(low_pair[:, 0], banks[0:R1, 1, 0:P], low_done, b + 1, low_hi, LORA1_SCALE)

            def stage_b(b, nxt):
                to_high(x2t_pair[:, 0].rearrange("p c n -> p (c n)"), banks[:, 3, :], x2t_done, b + 1, x2t_hi)
                if nxt is not None:
                    to_high(x1t_pair[:, 0].rearrange("p c n -> p (c n)"), banks[:, 0, :], x1t_done, nxt + 1, x1t_hi)
                act.wait_ge(gates, GSTEPS * b + 2)
                act.activation(expl[:], logits[:], ACT.Exp).then_inc(exp_done, 1)
                if nxt is not None:
                    to_high(low_pair[:, 0], banks[0:R1, 1, 0:P], low_done, nxt + 1, low_hi, LORA1_SCALE)
                to_high(hgt_pair[:, 0], banks[:, 5, 0:P], hgt_done, b + 1, hgt_hi)
                to_high(x3t_pair[:, 0, :, ds(b * S, S)], banks[:, 7, :].rearrange("p (c n) -> p c n", c=DC),
                        x3t_done, b + 1, x3t_hi)

            stage_a(0)
            to_high(w2_pair[:, 0].rearrange("p c n -> p (c n)"), w12_raw[:], s_w2, 16, w12_hi)
            with act.Fori(0, B - 1) as b:
                stage_b(b, b + 1)
            stage_b(B - 1, None)

            act.wait_ge(x3t_lo, B)
            act.wait_ge(s_ffs, 16 * 6 * B)
            act.activation(db_pair[:, 0], d_b[:], ACT.Copy).then_inc(db_hi, 1)
            for k in range(2):
                to_high(ga_pair[k][:, 0], ga_f[:, k], ga_got, k + 1, ga_hi)

            def fw_high(m, par):
                act.wait_ge(s_fwx[par], 16 * 3 * (m // 2 + 1))
                act.wait_ge(s_fw[par], 16 * 3 * (m // 2 + 1))
                if not (isinstance(m, int) and m < 2):
                    act.wait_ge(down_done, m - 1)
                act.activation(fw_pair[par][:, 0], fw_raw[par][:], ACT.Copy).then_inc(fw_hi, 1)

            def swish(m, par):
                act.wait_ge(g_done, m + 1)
                act.activation(sig[:], g_ps, ACT.Sigmoid).then_inc(sig_done, 1)
                to_high(act_pair[par][:, 0], act_f[:], act_done, m + 1, act_hi)

            fw_high(0, 0)
            for half in range(2):
                first = half * FT
                for k in range(2):
                    to_high(tg_pair[k][:, 0], own_f[:].rearrange("p b n -> p (b n)"), tg_own, 2 * half + k + 1, tg_hi)
                if half:
                    fw_high(first, first % 2)

                def ff_step(ft, par):
                    swish(first + ft - 1, 1 - par)
                    fw_high(first + ft, par)

                tiles(act, half, ff_step)
                swish(first + FT - 1, (first + FT - 1) % 2)
                to_high(td_pair[:, 0], own_f[:].rearrange("p b n -> p (b n)"), td_own, half + 1, td_hi)

        @block.vector
        def _(dve):
            def q_rope(n):
                b = n % B
                dve.wait_ge(q_copied, n + 1)
                if not (isinstance(n, int) and n == 0):
                    dve.wait_ge(qt_done, n)
                for k, dst in enumerate((q_cos, q_sin)):
                    tab = tabs[:, ds(b), k, :].broadcast_to([P, REP, D])
                    dve.tensor_tensor(dst[:], q_sb[:], tab, ALU.mult).then_inc(q_mul, 1)

            def k_rope(n, par):
                b = n % B
                dve.wait_ge(k_rsd, n + 1)
                if not (isinstance(n, int) and n == 0):
                    dve.wait_ge(k_rot, n)
                for k, dst in enumerate((k_cos, k_sin)):
                    dve.scalar_tensor_tensor(out=dst[:], in0=kv_raw[:, par, KC - 1, 0:D], scalar=k_rs[:, 0:1],
                                             in1=tabs[:, ds(b), 2 + k, :].rearrange("p a d -> p (a d)"),
                                             op0=ALU.mult, op1=ALU.mult).then_inc(k_mul, 1)

            def low(hi_sem, count, pair, src, lo_sem):
                dve.wait_ge(hi_sem, count)
                dve.tensor_tensor(pair[1], src, pair[0].bitcast(F32), ALU.subtract).then_inc(lo_sem, 1)

            def qt_low(n):
                low(qt_hi, n + 1, [qt_pair[:, k].rearrange("p h n -> p (h n)") for k in range(2)], q_ps, qt_lo)

            def kt_low(n):
                low(kt_hi, n + 1, [kt_pair[:, k] for k in range(2)], kt_ps, kt_lo)

            def o_low(n):
                low(o_hi, n + 1, [o_pair[:, k].rearrange("p h n -> p (h n)") for k in range(2)], misc_ps, o_lo)

            def pt_low(n, h):
                low(pt_hi, REP * n + h + 1, [pt_pair[:, k, h].rearrange("p c n -> p (c n)") for k in range(2)],
                    pt_ps, pt_lo)

            def mask_max(n, par, h):
                dve.wait_ge(scored, REP * n + h + 1)
                if h == 0:
                    dve.wait_ge(mask_done, n + 1)
                if not (isinstance(n, int) and n == 0):
                    dve.wait_ge(t_done, REP * (n - 1) + h + 1)
                settle(dve, 12 + h)
                two = prob[:, h, :].rearrange("p (a n) -> p a n", a=2)
                dve.tensor_tensor_reduce(out=two, in0=score_ps[h % 2][:, :, 0:HALF],
                                         in1=mask[:, par, :].rearrange("p (a n) -> p a n", a=2),
                                         scale=1.0, scalar=-3e38, op0=ALU.add, op1=ALU.max,
                                         accum_out=smax[:, h:h + 1]).then_inc(masked, 1)
                dve.wait_ge(masked, REP * n + h + 1)
                dve.wait_ge(q_rsd, n + 1)
                dve.tensor_scalar(nbias[:, h:h + 1], smax[:, h:h + 1], q_rs[par][:, h:h + 1], -1.0,
                                  ALU.mult, ALU.mult).then_inc(biased, 1)

            def normalise(n, h):
                dve.wait_ge(exped, REP * n + h + 1)
                dve.reciprocal(rsum[:, h:h + 1], psum_row[:, h:h + 1]).then_inc(recip, 1)
                dve.wait_ge(recip, REP * n + h + 1)
                dve.tensor_scalar(prob[:, h, :], prob[:, h, :], rsum[:, h:h + 1], None,
                                  ALU.mult).then_inc(normed, 1)

            def make_mask(n, par):
                if not (isinstance(n, int) and n < 2):
                    dve.wait_ge(masked, REP * (n - 1))
                dve.tensor_scalar(mask[:, par, 0:CACHE], iota[:], seq_f[:, ds(n % B)], NEG, ALU.is_ge,
                                  ALU.mult).then_inc(mask_done, 1)

            def w_high(m, par):
                dve.wait_ge(s_win[par], 16 * (m // 2 + 1))
                if not (isinstance(m, int) and m < PIECES):
                    dve.wait_ge(kvp_done, m - PIECES + 1)
                dve.tensor_scalar(w_pair[:, 0, ds((m % (2 * PIECES)) * PW, PW)], w_raw[:, par, :], 1.0, None,
                                  ALU.mult).then_inc(w_hi, 1)

            def add_attention(n):
                dve.wait_ge(wo_done, n + 1)
                dst = acc[:, ds(n % B), :].rearrange("p a n -> p (a n)")
                dve.tensor_tensor(dst, misc_ps, dst, ALU.add).then_inc(added, 1)

            dve.wait_ge(s_trig, 16 * (B + 1))
            h = D // 2
            cos, sin = trig[:, :, 0:h], trig[:, :, h:D]
            for k in range(2):
                scale = 1.0 if k == 0 else float(D) ** 0.5
                for j, (src, sign, tab) in enumerate(((cos, 1, 0), (cos, 1, 0), (sin, 1, 1), (sin, -1, 1))):
                    half = slice(h * (j % 2), h * (j % 2) + h)
                    last = dve.scalar_tensor_tensor(
                        out=tabs[:, :, 2 * k + tab, half], in0=src, scalar=sign * scale,
                        in1=wnorm[:, k, half].unsqueeze(1).broadcast_to([P, B, h]), op0=ALU.mult, op1=ALU.mult)
            last.then_inc(tab_done, 1)
            dve.wait_ge(s_const, 48)
            dve.tensor_copy(seq_f[:], seq_i[:]).then_inc(seq_done, 1)
            for m in range(QKV_PIECES):
                w_high(m, m % 2)
            dve.wait_ge(seq_done, 1)
            dve.wait_ge(halves, 1)
            make_mask(0, 0)
            dve.wait_ge(tab_done, 1)
            k_rope(0, 0)
            q_rope(0)
            for m in range(QKV_PIECES, PIECES):
                w_high(m, m % 2)
            kt_low(0)
            qt_low(0)
            dve.wait_ge(s_acc0, 16)

            def step(n, par, x=True, w=True, nxt=True):
                first = isinstance(n, int) and n == 0
                mask_max(n, par, 0)
                mask_max(n, par, 1)
                normalise(n, 0)
                normalise(n, 1)
                if w:
                    w_high(n + PIECES, par)
                if nxt:
                    make_mask(n + 1, 1 - par)
                if not first:
                    o_low(n - 1)
                mask_max(n, par, 2)
                pt_low(n, 0)
                normalise(n, 2)
                if nxt:
                    k_rope(n + 1, 1 - par)
                pt_low(n, 1)
                if nxt:
                    q_rope(n + 1)
                mask_max(n, par, 3)
                if nxt:
                    kt_low(n + 1)
                pt_low(n, 2)
                normalise(n, 3)
                if nxt:
                    qt_low(n + 1)
                if not first:
                    add_attention(n - 1)
                pt_low(n, 3)

            steps(dve, step)
            o_low(NT - 1)
            add_attention(NT - 1)

            def flat(ap):
                return ap.rearrange("p c n -> p (c n)")

            low(w12_hi, 1, [flat(w1_pair[:, k]) for k in range(2)], w12_raw[:], w12_lo)
            dve.wait_ge(sm_hi, 1)
            dve.tensor_tensor(b1_pair[:, 1], b1_raw[:], b1_pair[:, 0].bitcast(F32), ALU.subtract)
            dve.tensor_tensor(ra_pair[:, 1], ra_raw[:], ra_pair[:, 0].bitcast(F32), ALU.subtract)
            dve.tensor_tensor(b2_pair[:, 1], b2_raw[:], b2_pair[:, 0].bitcast(F32), ALU.subtract).then_inc(sm_lo, 1)
            dve.tensor_copy(lang_f[:], lang_i[:]).then_inc(lang_done, 1)
            dve.wait_ge(lang_done, 1)
            for b in range(B):
                last = dve.tensor_scalar(lbias[:, b, :], experts[:], lang_f[:, b:b + 1], LANG_BIAS,
                                         ALU.is_equal, ALU.mult)
            last.then_inc(lbias_done, 1)
            dve.wait_ge(s_a1, 16 * B)
            dve.wait_ge(a1_zero, 1)

            def begin_a(b):
                if not (isinstance(b, int) and b == 0):
                    dve.wait_ge(low_done, b)
                    dve.wait_ge(x2_done, b)
                dve.tensor_scalar(a1_pair[:, 0, :, 0:R1], a1_raw[:, ds(b), :, :].rearrange("p b c r -> p (b c) r"),
                                  1.0, None, ALU.mult).then_inc(a1_hi, 1)
                dve.tensor_scalar(x1_sb[:], acc[:, ds(b), :].rearrange("p b n -> p (b n)"), 1.0, None,
                                  ALU.mult).then_inc(x1_done, 1)

            def x1t_low(b):
                low(x1t_hi, b + 1, [flat(x1t_pair[:, k]) for k in range(2)], banks[:, 0, :], x1t_lo)

            def lora1_low(b):
                dve.wait_ge(low_hi, b + 1)
                dve.scalar_tensor_tensor(out=low_pair[:, 1], in0=banks[0:R1, 1, 0:P], scalar=LORA1_SCALE,
                                         in1=low_pair[:, 0].bitcast(F32), op0=ALU.mult,
                                         op1=ALU.subtract).then_inc(low_lo, 1)

            def end_a(b):
                dve.wait_ge(y1_done, b + 1)
                dve.tensor_tensor(x2_sb[:], banks[:, 2, :], x1_sb[:], ALU.add).then_inc(x2_done, 1)

            def gate_start(b):
                n = GSTEPS * b
                dve.wait_ge(hl_done, b + 1)
                dve.tensor_tensor(logits[:], banks[:, 4, 0:E], lbias[:, ds(b), :].rearrange("p b e -> p (b e)"),
                                  ALU.add).then_inc(gates, 1)
                dve.wait_ge(gates, n + 1)
                dve.tensor_reduce(top[:], logits[:], mybir.AxisListType.X, ALU.max).then_inc(top_done, 1)
                dve.wait_ge(top_done, b + 1)
                dve.tensor_scalar(logits[:], logits[:], top[:], None, ALU.subtract).then_inc(gates, 1)

            def gate_end(b):
                n = GSTEPS * b
                every = logits[:].unsqueeze(1).broadcast_to([P, E, E])
                own = logits[:].unsqueeze(2).broadcast_to([P, E, E])
                dve.wait_ge(gates, n + 2)
                dve.tensor_tensor(above[:], every, own, ALU.is_gt)
                dve.tensor_tensor(equal[:], every, own, ALU.is_equal).then_inc(gates, 1)
                dve.wait_ge(gates, n + 3)
                dve.tensor_tensor(equal[:], equal[:], lower[:], ALU.mult).then_inc(gates, 1)
                dve.wait_ge(gates, n + 4)
                dve.tensor_tensor(above[:], above[:], equal[:], ALU.add).then_inc(gates, 1)
                dve.wait_ge(gates, n + 5)
                dve.tensor_reduce(rank[:], above[:], mybir.AxisListType.X, ALU.add).then_inc(gates, 1)
                dve.wait_ge(gates, n + 6)
                dve.wait_ge(exp_done, b + 1)
                dve.scalar_tensor_tensor(out=gate[:], in0=rank[:], scalar=1.5, in1=expl[:], op0=ALU.is_lt,
                                         op1=ALU.mult).then_inc(gates, 1)
                dve.wait_ge(gates, n + 7)
                dve.tensor_reduce(gsum[:], gate[:], mybir.AxisListType.X, ALU.add).then_inc(gates, 1)
                dve.wait_ge(gates, n + 8)
                dve.reciprocal(grec[:], gsum[:]).then_inc(gates, 1)
                dve.wait_ge(gates, n + 9)
                dve.tensor_scalar(gate[:], gate[:], grec[:], LORA2_SCALE, ALU.mult, ALU.mult).then_inc(gates, 1)
                dve.wait_ge(gates, n + 10)
                dve.tensor_tensor(hg[:], banks[:, 4, E:E + ER].rearrange("p (e r) -> p e r", e=E),
                                  gate[:].unsqueeze(2).broadcast_to([P, E, R2]), ALU.mult).then_inc(gates, 1)

            def end_b(b):
                dve.wait_ge(y2_done, b + 1)
                if not (isinstance(b, int) and b == 0):
                    dve.wait_ge(x3_kept, b)
                dve.tensor_tensor(x3_sb[:], banks[:, 6, :], x2_sb[:], ALU.add).then_inc(x3_done, 1)
                dve.wait_ge(x3_done, b + 1)
                dve.tensor_scalar(acc[:, ds(b), :].rearrange("p b n -> p (b n)"), x3_sb[:], 1.0, None,
                                  ALU.mult).then_inc(x3_kept, 1)

            def stage_b(b, nxt):
                if nxt is not None:
                    begin_a(nxt)
                low(x2t_hi, b + 1, [flat(x2t_pair[:, k]) for k in range(2)], banks[:, 3, :], x2t_lo)
                if nxt is not None:
                    x1t_low(nxt)
                gate_start(b)
                gate_end(b)
                if nxt is not None:
                    lora1_low(nxt)
                low(hgt_hi, b + 1, [hgt_pair[:, k] for k in range(2)], banks[:, 5, 0:P], hgt_lo)
                end_b(b)
                if nxt is not None:
                    end_a(nxt)
                low(x3t_hi, b + 1, [x3t_pair[:, k, :, ds(b * S, S)] for k in range(2)],
                    banks[:, 7, :].rearrange("p (c n) -> p c n", c=DC), x3t_lo)

            begin_a(0)
            x1t_low(0)
            low(w12_hi, 2, [flat(w2_pair[:, k]) for k in range(2)], w12_raw[:], w12_lo)
            lora1_low(0)
            end_a(0)
            with dve.Fori(0, B - 1) as b:
                stage_b(b, b + 1)
            stage_b(B - 1, None)

            dve.wait_ge(s_ffs, 16 * 6 * B)
            for k in range(2):
                for c in range(DC):
                    last = dve.tensor_copy(ga_f[:, k, c].rearrange("p (b r) -> p b r", b=B),
                                           gu_a[:, k, :, c * R3:(c + 1) * R3])
                last.then_inc(ga_got, 1)
            low(db_hi, 1, [db_pair[:, k] for k in range(2)], d_b[:], db_lo)
            for k in range(2):
                low(ga_hi, k + 1, [ga_pair[k][:, j] for j in range(2)], ga_f[:, k], ga_lo)

            def own(src, half):
                return dve.tensor_tensor(own_f[:], src.rearrange("p (b n) -> p b n", b=HB),
                                         own_rows[:, half * HB:(half + 1) * HB].unsqueeze(2).broadcast_to([P, HB, S]),
                                         ALU.mult)

            def gated(m, par):
                dve.wait_ge(sig_done, m + 1)
                dve.tensor_tensor(gsig[:], g_ps, sig[:], ALU.mult).then_inc(gsig_done, 1)
                dve.wait_ge(gsig_done, m + 1)
                dve.wait_ge(u_done, m + 1)
                if not (isinstance(m, int) and m == 0):
                    dve.wait_ge(act_lo, m)
                dve.tensor_tensor(act_f[:], u_ps, gsig[:], ALU.mult).then_inc(act_done, 1)
                low(act_hi, m + 1, [act_pair[par][:, k] for k in range(2)], act_f[:], act_lo)

            for half in range(2):
                first = half * FT
                for k in range(2):
                    dve.wait_ge(tg_done, 2 * half + k + 1)
                    if k:
                        dve.wait_ge(tg_lo, 2 * half + k)
                    elif half:
                        dve.wait_ge(td_lo, half)
                    own(t_ps, half).then_inc(tg_own, 1)
                    low(tg_hi, 2 * half + k + 1, [tg_pair[k][:, j] for j in range(2)],
                        own_f[:].rearrange("p b n -> p (b n)"), tg_lo)
                tiles(dve, half, lambda ft, par: gated(first + ft - 1, 1 - par))
                gated(first + FT - 1, (first + FT - 1) % 2)
                dve.wait_ge(down_done, first + FT)
                dve.wait_ge(tg_lo, 2 * half + 2)
                own(t_ps, half).then_inc(td_own, 1)
                low(td_hi, half + 1, [td_pair[:, j] for j in range(2)], own_f[:].rearrange("p b n -> p (b n)"), td_lo)
                for j in range(HB):
                    b = half * HB + j
                    dve.wait_ge(ffn_done, b + 1)
                    dve.tensor_tensor(acc[:, b, :], ffn_bank[j], acc[:, b, :], ALU.add).then_inc(ffn_added, 1)

        @block.tensor
        def _(pe):
            def group_at(n):
                return ((n // B) % 2) * GW

            def project_q(n, par, part):
                if part == 0 and not (isinstance(n, int) and n == 0):
                    pe.wait_ge(qt_lo, n)
                at = group_at(n)
                for c in range(2 * part, 2 * part + 2):
                    last = product(pe, q_ps, lambda k: x_pair[par][:, k, c, :],
                                   lambda k: w_pair[:, k, ds(at + c * REP * P, REP * P)], c == 0, c == DC - 1)
                if part == 1:
                    last.then_inc(q_done, 1)

            def project_kv(n, par):
                pe.wait_ge(x_lo, n + 1)
                pe.wait_ge(w_lo, (n // B) * PIECES + QKV_PIECES)
                if isinstance(n, int) and n == 1:
                    pe.wait_ge(kv_copied, 1)
                elif not (isinstance(n, int) and n == 0):
                    pe.wait_ge(o_lo, n - 1)
                at = group_at(n) + WKV
                for c in range(DC):
                    last = product(pe, misc_ps[:, 0:2 * D], lambda k: x_pair[par][:, k, c, :],
                                   lambda k: w_pair[:, k, ds(at + c * 2 * D, 2 * D)], c == 0, c == DC - 1)
                last.then_inc(kvp_done, 1)

            def transpose_q(n):
                pe.wait_ge(q_rot, n + 1)
                pe.wait_ge(q_sq, n + 1)
                for h in range(REP):
                    last = pe.transpose(q_ps[:, h * P:(h + 1) * P], q_cos[:, h, :], ident[:])
                last.then_inc(qt_done, 1)

            def transpose_cached_k(n, par):
                pe.wait_ge(s_kvin[par], 16 * NPP * (n // 2 + 1))
                if not (isinstance(n, int) and n == 0):
                    pe.wait_ge(masked, REP * (n - 1) + 3)
                for c in range(KC - 1):
                    pe.transpose(kt_ps[:, c * P:(c + 1) * P], kv_raw[:, par, c, 0:D], ident[:])

            def transpose_new_k(n, par):
                pe.wait_ge(k_rot, n + 1)
                pe.transpose(kt_ps[:, CACHE:KEYS], kv_raw[:, par, KC - 1, 0:D], ident[:]).then_inc(kt_done, 1)

            def scores(n, h):
                if h == 0:
                    pe.wait_ge(qt_lo, n + 1)
                    pe.wait_ge(kt_lo, n + 1)
                elif h > 1:
                    pe.wait_ge(masked, REP * n + h - 1)
                elif not (isinstance(n, int) and n == 0):
                    pe.wait_ge(masked, REP * n)
                for a in range(2):
                    last = product(pe, score_ps[h % 2][:, a, 0:HALF], lambda k: qt_pair[:, k, h, :],
                                   lambda k: kt_pair[:, k, a * HALF:(a + 1) * HALF], True, True)
                last.then_inc(scored, 1)

            def transpose_p(n, h):
                pe.wait_ge(normed, REP * n + h + 1)
                if not (isinstance(n, int) and n == 0 and h == 0):
                    pe.wait_ge(pt_lo, REP * n + h)
                for c in range(KC):
                    last = pe.transpose(pt_ps[:, c * P:(c + 1) * P], prob[:, h, c * P:(c + 1) * P], ident[:])
                last.then_inc(t_done, 1)

            def values(n, par):
                pe.wait_ge(pt_lo, REP * (n + 1))
                pe.wait_ge(v_lo, n + 1)
                for c in range(KC):
                    last = product(pe, misc_ps.rearrange("p (h n) -> p h n", h=REP),
                                   lambda k: v_pair[par][:, k, c, :], lambda k: pt_pair[:, k, :, c, :],
                                   c == 0, c == KC - 1)
                last.then_inc(pv_done, 1)

            def project_out(n, part, steady=True):
                if part == 0:
                    pe.wait_ge(o_lo, n + 1)
                    if steady:
                        pe.wait_ge(kv_copied, n + 3)
                    pe.wait_ge(w_lo, (n // B) * PIECES + PIECES)
                at = group_at(n) + WWO
                for h in range(2 * part, 2 * part + 2):
                    last = product(pe, misc_ps, lambda k: o_pair[:, k, h, :],
                                   lambda k: w_pair[:, k, ds(at + h * HID, HID)], h == 0, h == REP - 1)
                if part == 1:
                    last.then_inc(wo_done, 1)

            def step(n, par, x=True, w=True, nxt=True):
                first = isinstance(n, int) and n == 0
                scores(n, 0)
                scores(n, 1)
                if not first:
                    values(n - 1, 1 - par)
                scores(n, 2)
                transpose_p(n, 0)
                if nxt:
                    project_kv(n + 1, 1 - par)
                    project_q(n + 1, 1 - par, 0)
                transpose_p(n, 1)
                if nxt:
                    project_q(n + 1, 1 - par, 1)
                scores(n, 3)
                if nxt:
                    transpose_cached_k(n + 1, 1 - par)
                    transpose_new_k(n + 1, 1 - par)
                transpose_p(n, 2)
                if not first:
                    project_out(n - 1, 0, nxt)
                if nxt:
                    transpose_q(n + 1)
                if not first:
                    project_out(n - 1, 1)
                transpose_p(n, 3)

            pe.wait_ge(s_const, 48)
            project_kv(0, 0)
            project_q(0, 0, 0)
            project_q(0, 0, 1)
            transpose_cached_k(0, 0)
            transpose_new_k(0, 0)
            transpose_q(0)
            steps(pe, step)
            values(NT - 1, 1)
            project_out(NT - 1, 0, False)
            project_out(NT - 1, 1)

            def transpose4(bank, src):
                for c in range(DC):
                    last = pe.transpose(bank[:, c * P:(c + 1) * P], src[:, c * P:(c + 1) * P], ident[:])
                return last

            def linear(dst, xt, w, stop):
                for c in range(DC):
                    last = product(pe, dst, lambda k: xt[:, k, c, :], lambda k: w[:, k, c, :], c == 0,
                                   stop and c == DC - 1)
                return last

            def x1_transpose(b):
                pe.wait_ge(x1_done, b + 1)
                transpose4(banks[:, 0, :], x1_sb).then_inc(x1t_done, 1)

            def lora1(b):
                pe.wait_ge(x1t_lo, b + 1)
                pe.wait_ge(a1_lo, b + 1)
                for c in range(DC):
                    last = product(pe, banks[:, 1, 0:P], lambda k: a1_pair[:, k, c, :], lambda k: x1t_pair[:, k, c, :],
                                   c == 0, c == DC - 1)
                last.then_inc(low_done, 1)

            def block1(b):
                linear(banks[:, 2, :], x1t_pair, w1_pair, False)
                pe.wait_ge(low_lo, b + 1)
                product(pe, banks[:, 2, :], lambda k: low_pair[:, k, :], lambda k: b1_pair[:, k, :],
                        False, True).then_inc(y1_done, 1)

            def stage_b(b, nxt):
                pe.wait_ge(x2_done, b + 1)
                transpose4(banks[:, 3, :], x2_sb).then_inc(x2t_done, 1)
                if nxt is not None:
                    x1_transpose(nxt)
                pe.wait_ge(x2t_lo, b + 1)
                linear(banks[:, 4, 0:E + ER], x2t_pair, ra_pair, True).then_inc(hl_done, 1)
                if nxt is not None:
                    lora1(nxt)
                linear(banks[:, 6, :], x2t_pair, w2_pair, False)
                pe.wait_ge(gates, GSTEPS * b + GSTEPS)
                pe.transpose(banks[:, 5, 0:P], hg[:].rearrange("p e r -> p (e r)"), ident[:]).then_inc(hgt_done, 1)
                if nxt is not None:
                    linear(banks[:, 2, :], x1t_pair, w1_pair, False)
                pe.wait_ge(hgt_lo, b + 1)
                product(pe, banks[:, 6, :], lambda k: hgt_pair[:, k, :], lambda k: b2_pair[:, k, :],
                        False, True).then_inc(y2_done, 1)
                if nxt is not None:
                    pe.wait_ge(low_lo, nxt + 1)
                    product(pe, banks[:, 2, :], lambda k: low_pair[:, k, :], lambda k: b1_pair[:, k, :],
                            False, True).then_inc(y1_done, 1)
                pe.wait_ge(x3_done, b + 1)
                transpose4(banks[:, 7, :], x3_sb).then_inc(x3t_done, 1)

            x1_transpose(0)
            lora1(0)
            pe.wait_ge(w12_lo, 1)
            pe.wait_ge(sm_lo, 1)
            block1(0)
            pe.wait_ge(w12_lo, 2)
            with pe.Fori(0, B - 1) as b:
                stage_b(b, b + 1)
            stage_b(B - 1, None)

            pe.wait_ge(x3t_lo, B)
            for half in range(2):
                first = half * FT
                tokens = slice(half * HT, (half + 1) * HT)
                for k in range(2):
                    if half == 0:
                        pe.wait_ge(ga_lo, k + 1)
                    if half or k:
                        pe.wait_ge(tg_own if k else td_own, 2 * half + k if k else half)
                    for c in range(DC):
                        last = product(pe, t_ps, lambda j: ga_pair[k][:, j, c, :], lambda j: x3t_pair[:, j, c, tokens],
                                       c == 0, c == DC - 1)
                    last.then_inc(tg_done, 1)

                def gate_up(m, par):
                    pe.wait_ge(fw_lo, m + 1)
                    for k, dst, at, at_b, sem_read, sem_done in ((0, g_ps, F_GATE, F_GATE_B, gsig_done, g_done),
                                                                 (1, u_ps, F_UP, F_UP_B, act_done, u_done)):
                        if not (isinstance(m, int) and m == 0):
                            pe.wait_ge(sem_read, m)
                        for c in range(DC):
                            product(pe, dst, lambda j: fw_pair[par][:, j, at + c * P:at + (c + 1) * P],
                                    lambda j: x3t_pair[:, j, c, tokens], c == 0, False)
                        if isinstance(m, int) and m == first:
                            pe.wait_ge(tg_lo, 2 * half + k + 1)
                        product(pe, dst, lambda j: fw_pair[par][:, j, at_b:at_b + P], lambda j: tg_pair[k][:, j, :],
                                False, True).then_inc(sem_done, 1)

                def down(m, par, start, stop):
                    pe.wait_ge(act_lo, m + 1)
                    if start and half:
                        pe.wait_ge(ffn_added, HB)
                    for j in range(HB):
                        product(pe, ffn_bank[j], lambda k: act_pair[par][:, k, j * S:(j + 1) * S],
                                lambda k: fw_pair[par][:, k, F_DOWN:F_DOWN_A], start, False)
                    product(pe, t_ps, lambda k: fw_pair[par][:, k, F_DOWN_A:FW], lambda k: act_pair[par][:, k, :],
                            start, stop).then_inc(down_done, 1)

                def ff_step(ft, par):
                    gate_up(first + ft, par)
                    down(first + ft - 1, 1 - par, isinstance(ft, int) and ft == 1, False)

                gate_up(first, first % 2)
                tiles(pe, half, ff_step)
                down(first + FT - 1, (first + FT - 1) % 2, False, True)
                pe.wait_ge(td_lo, half + 1)
                if half == 0:
                    pe.wait_ge(db_lo, 1)
                for j in range(HB):
                    product(pe, ffn_bank[j], lambda k: td_pair[:, k, j * S:(j + 1) * S], lambda k: db_pair[:, k, :],
                            False, True).then_inc(ffn_done, 1)


def rope_rows():
    inv = (1.0 / 10000.0 ** (np.arange(0, D, 2, dtype=np.float64) / D)).astype(np.float32)
    pos = np.arange(POS_END - 1 + S, dtype=np.float32)
    angle = (pos[:, None] * inv[None, :]).astype(np.float64)
    return np.concatenate([np.cos(angle), np.sin(angle)], 1).astype(np.float32)


def kernel(**inputs):
    import concourse.bacc as _bacc
    from concourse.bass_utils import run_bass_kernel_spmd as _run

    i = {k: np.asarray(v) for k, v in inputs.items()}
    x = i["x"]

    def by_partition(w, cols):
        return w.reshape(cols, DC, P).transpose(2, 1, 0)

    wq = i["L0_cond_Wq"].reshape(HK, REP * D, DC, P).transpose(0, 3, 2, 1).reshape(HK, P, -1)
    wk = i["L0_cond_Wk"].reshape(HK, D, DC, P).transpose(0, 3, 2, 1)
    wv = i["L0_cond_Wv"].reshape(HK, D, DC, P).transpose(0, 3, 2, 1)
    wkv = np.stack([wk, wv], 3).reshape(HK, P, -1)
    wo = i["L0_cond_Wo"].reshape(HID, HK, REP, D).transpose(1, 3, 2, 0).reshape(HK, P, -1)
    w_att = np.concatenate([wq, wkv, wo], 2).reshape(HK, P, PIECES, PW).transpose(0, 2, 1, 3).reshape(NT, P, PW)
    kv = np.stack([i["L0_cond_k_cache"], i["L0_cond_v_cache"]], 3)
    kv = kv.transpose(2, 0, 1, 3, 4).reshape(HK, PAGES, PSIZE, 2 * D)
    arrays = {
        "x": x,
        "xT": x.reshape(B, S, DC, P).transpose(0, 3, 2, 1).reshape(B, P, DC * S),
        "w_att": w_att,
        "kv": kv,
        "wnorm": np.stack([i["L0_cond_q_norm_w"], i["L0_cond_k_norm_w"]]),
        "pages": i["itok_Bx16_0_63"],
        "seqlens": i["itok_B_207_1644"],
        "trig": rope_rows(),
        "ident": np.eye(P, dtype=np.float32),
        "iota": np.arange(CACHE, dtype=np.float32),
    }
    w12 = np.stack([by_partition(i[k], HID).reshape(P, -1) for k in ("L1_cond_weight", "L2_cond_W")])
    ra = np.concatenate([by_partition(i["L2_cond_Wr"], E), by_partition(i["L2_cond_A"].reshape(ER, HID), ER)], 2)

    def padded(a, axis):
        wide = [(0, 0)] * a.ndim
        wide[axis] = (0, FP - F)
        return np.pad(a, wide)

    gate_w, up_w = (padded(i[k], 0).reshape(FT, P, DC, P).transpose(0, 3, 2, 1).reshape(FT, P, DC * P)
                    for k in ("L3_cond_W_gate", "L3_cond_W_up"))
    down_w = padded(i["L3_cond_W_down"], 1).reshape(HID, FT, P).transpose(1, 2, 0)
    arrays.update({
        "w12": w12,
        "a1": i["L1_cond_lora_A"].reshape(-1, DC, P, R1).transpose(0, 2, 1, 3).reshape(-1, P, DC * R1),
        "b1": i["L1_cond_lora_B_w"].T,
        "ra": ra.reshape(P, -1),
        "b2": i["L2_cond_B"].transpose(0, 2, 1).reshape(ER, HID),
        "label": i["itok_B_0_4"], "lang": i["itok_B_0_7"], "lora": i["itok_B_2_6"],
        "experts": np.arange(E, dtype=np.float32),
        "lower": np.tril(np.ones((E, E), np.float32), -1).reshape(-1),
        "own": np.kron(np.eye(B), np.full((R3, 1), LORA3_SCALE)).astype(np.float32),
        "gu_a": np.stack([i[k][0].reshape(-1, R3, DC, P).transpose(0, 3, 2, 1).reshape(-1, P, DC * R3)
                          for k in ("L3_cond_A_gate", "L3_cond_A_up")]),
        "gu_b": np.stack([padded(i[k][0], 1).transpose(0, 2, 1) for k in ("L3_cond_B_gate", "L3_cond_B_up")]),
        "d_a": padded(i["L3_cond_A_down"][0], 2).reshape(-1, R3, FT, P).transpose(0, 3, 2, 1),
        "d_b": i["L3_cond_B_down"][0].transpose(0, 2, 1),
        "fw": np.stack([gate_w, up_w, down_w]),
    })
    nc = _bacc.Bacc("TRN2", target_bir_lowering=False, num_devices=1)
    arrays = {k: np.ascontiguousarray(v) for k, v in arrays.items()}
    t = {k: nc.dram_tensor(f"in_{k}", v.shape, mybir.dt.from_np(v.dtype), kind="ExternalInput").ap()
         for k, v in arrays.items()}
    out = nc.dram_tensor("out_x", (B, S, HID), F32, kind="ExternalOutput").ap()
    build(nc, t, out)
    r = _run(nc, [{f"in_{k}": v for k, v in arrays.items()}], core_ids=[0])
    return r.results[0]["out_x"]
```

```python
from contextlib import ExitStack

import numpy as np

import concourse.bass as bass
from concourse import mybir

F32 = mybir.dt.float32
F32R = mybir.dt.float32r
I32 = mybir.dt.int32
ALU = mybir.AluOpType
ACT = mybir.ActivationFunctionType

P = 128
B, S, HID = 8, 128, 512
D, HQ, HK = 128, 32, 8
REP = HQ // HK
PAGES, PSIZE, NPP = 64, 32, 16
CACHE = NPP * PSIZE
KEYS = CACHE + S
KC = KEYS // P
HALF = KEYS // 2
DC = HID // P
NT = HK * B
GW = (REP * DC + 2 * DC + REP * DC) * P
PIECES = 8
PW = GW // PIECES
WKV = REP * DC * P
WWO = WKV + 2 * DC * P
QKV_PIECES = -(-WWO // PW)
POS_END = 1645
EPS = 1e-6
NEG = -1e30

R1 = 32
LORA1_SCALE = 0.5
E, R2 = 8, 16
LANG_BIAS, LORA2_SCALE = 5.0, 2.0
ER = E * R2
F, R3 = 1376, 16
BR = B * R3
LORA3_SCALE = 0.5
FT = -(-F // P)
FP = FT * P
HB = B // 2
HT = HB * S
FW = (DC + 1) * P * 2 + HID + P
GU, DN = slice(0, 1280), slice(1280, 1920)
F_GATE, F_GATE_B, F_UP, F_UP_B, F_DOWN, F_DOWN_A = 0, 512, 640, 1152, 1280, 1792


def ds(i, n=1):
    return bass.ds(i, n)


def build(nc, t, out):
    ctx = ExitStack()
    with ctx:
        def sb(name, shape, dt=F32, where=ctx):
            return where.enter_context(nc.sbuf_tensor(name, shape, dt))

        def sem(name):
            return ctx.enter_context(nc.semaphore(name))

        ident = sb("ident", [P, P])
        spare = sb("spare", [P, 16])
        acc = sb("acc", [P, B, HID])

        banks = ctx.enter_context(nc.psum_tensor("banks", [P, 8, 512], F32))
        score_ps = [banks[:, 0:2, :], banks[:, 2:4, :]]
        pt_ps = banks[:, 4:6, :].rearrange("p a n -> p (a n)")[:, 0:KEYS]
        q_ps = banks[:, 6, :]
        misc_ps = banks[:, 7, :]
        kt_ps = banks[:, 0:2, :].rearrange("p a n -> p (a n)")[:, 0:KEYS]

        att = ExitStack()
        w_pair = sb("w_pair", [P, 2, 2 * GW], F32R, where=att)
        tabs = sb("tabs", [P, B, 4, P], where=att)
        iota = sb("iota", [P, CACHE], where=att)
        mask = sb("mask", [P, 2, KEYS], where=att)
        seq_i = sb("seq_i", [P, B], I32, where=att)
        seq_f = sb("seq_f", [P, B], where=att)
        half_neg = sb("half_neg", [P, REP], where=att)
        w_raw = sb("w_raw", [P, 2, PW], where=att)
        x_raw = sb("x_raw", [P, 2, DC * P], where=att)
        x_pair = [sb(f"x_pair{i}", [P, 2, DC, P], F32R, where=att) for i in range(2)]
        kv_raw = sb("kv_raw", [P, 2, KC, 2 * D], where=att)
        v_pair = [sb(f"v_pair{i}", [P, 2, KC, D], F32R, where=att) for i in range(2)]
        kt_pair = sb("kt_pair", [P, 2, KEYS], F32R, where=att)
        qt_pair = sb("qt_pair", [P, 2, REP, P], F32R, where=att)
        pt_pair = sb("pt_pair", [P, 2, REP, KC, P], F32R, where=att)
        o_pair = sb("o_pair", [P, 2, REP, P], F32R, where=att)
        prob = sb("prob", [P, REP, KEYS], where=att)
        q_sb = sb("q_sb", [P, REP, P], where=att)
        q_cos = sb("q_cos", [P, REP, P], where=att)
        q_sin = sb("q_sin", [P, REP, P], where=att)
        k_cos = sb("k_cos", [P, P], where=att)
        k_sin = sb("k_sin", [P, P], where=att)
        squares = sb("squares", [P, P], where=att)
        q_ss = sb("q_ss", [P, REP], where=att)
        q_se = sb("q_se", [P, REP], where=att)
        q_rs = [sb(f"q_rs{i}", [P, REP], where=att) for i in range(2)]
        k_ss = sb("k_ss", [P, 1], where=att)
        k_se = sb("k_se", [P, 1], where=att)
        k_rs = sb("k_rs", [P, 1], where=att)
        smax = sb("smax", [P, REP], where=att)
        nbias = sb("nbias", [P, REP], where=att)
        psum_row = sb("psum_row", [P, REP], where=att)
        rsum = sb("rsum", [P, REP], where=att)
        trig = prob[:, 0:2, :].rearrange("p a n -> p (a n)")[:, 0:B * D].rearrange("p (b d) -> p b d", b=B)
        wnorm = prob[:, 2, 0:2 * D].rearrange("p (a d) -> p a d", a=2)

        att.close()

        w1_raw = sb("w1_raw", [P, DC * HID])
        w2_raw = sb("w2_raw", [P, DC * HID])
        a1_raw = sb("a1_raw", [P, B, DC, R1])
        w2_pair = sb("w2_pair", [P, 2, DC, HID], F32R)
        d_b = sb("d_b", [P, HID])
        b1_raw = sb("b1_raw", [P, HID])
        w1_pair = sb("w1_pair", [P, 2, DC, HID], F32R)
        a1_pair = sb("a1_pair", [P, 2, DC, P], F32R)
        gu_b = sb("gu_b", [P, 2, FP])
        d_a = sb("d_a", [P, FT, BR])
        gu_a = sb("gu_a", [P, 2, B, DC * R3])
        x3t_pair = sb("x3t_pair", [P, 2, DC, B * S], F32R)
        own_rows = sb("own_rows", [P, B])
        ga_f = sb("ga_f", [P, 2, DC, BR])
        ga_pair = [sb(f"ga_pair{i}", [P, 2, DC, BR], F32R) for i in range(2)]
        tg_pair = [sb(f"tg_pair{i}", [P, 2, HT], F32R) for i in range(2)]
        fw_pair0 = sb("fw_pair0", [P, 2, FW], F32R)
        own_f = sb("own_f", [P, HB, S])
        mix = ExitStack()
        b1_pair = sb("b1_pair", [R1, 2, HID], F32R, where=mix)
        ra_raw = sb("ra_raw", [P, DC, E + ER], where=mix)
        ra_pair = sb("ra_pair", [P, 2, DC, E + ER], F32R, where=mix)
        b2_raw = sb("b2_raw", [P, HID], where=mix)
        b2_pair = sb("b2_pair", [P, 2, HID], F32R, where=mix)
        x1_sb = sb("x1_sb", [P, HID], where=mix)
        x2_sb = sb("x2_sb", [P, HID], where=mix)
        x3_sb = sb("x3_sb", [P, HID], where=mix)
        x1t_pair = sb("x1t_pair", [P, 2, DC, P], F32R, where=mix)
        x2t_pair = sb("x2t_pair", [P, 2, DC, P], F32R, where=mix)
        low_pair = sb("low_pair", [R1, 2, P], F32R, where=mix)
        hg = sb("hg", [P, E, R2], where=mix)
        hgt_pair = sb("hgt_pair", [P, 2, P], F32R, where=mix)
        lang_i = sb("lang_i", [P, B], I32, where=mix)
        lang_f = sb("lang_f", [P, B], where=mix)
        experts = sb("experts", [P, E], where=mix)
        lower = sb("lower", [P, E, E], where=mix)
        lbias = sb("lbias", [P, B, E], where=mix)
        logits = sb("logits", [P, E], where=mix)
        top = sb("top", [P, 1], where=mix)
        above = sb("above", [P, E, E], where=mix)
        equal = sb("equal", [P, E, E], where=mix)
        rank = sb("rank", [P, E], where=mix)
        expl = sb("expl", [P, E], where=mix)
        gate = sb("gate", [P, E], where=mix)
        gsum = sb("gsum", [P, 1], where=mix)
        grec = sb("grec", [P, 1], where=mix)
        mix.close()
        fw_raw = [w2_raw[:, 0:FW], w1_raw[:, 0:FW]]
        fw_pair = [fw_pair0, sb("fw_pair1", [P, 2, FW], F32R)]
        db_pair = sb("db_pair", [P, 2, HID], F32R)
        td_pair = sb("td_pair", [P, 2, HT], F32R)
        sig = sb("sig", [P, HT])
        gsig = sb("gsig", [P, HT])
        act_f = sb("act_f", [P, HT])
        act_pair = [sb(f"act_pair{i}", [P, 2, HT], F32R) for i in range(2)]
        ffn_bank = [banks[:, j, :] for j in range(HB)]
        t_ps, g_ps, u_ps, tg_ps = (banks[:, j, :] for j in range(4, 8))

        s_const = sem("s_const")
        s_trig = sem("s_trig")
        s_acc0 = sem("s_acc0")
        s_xin = [sem(f"s_xin{i}") for i in range(2)]
        s_win = [sem(f"s_win{i}") for i in range(2)]
        s_kvin = [sem(f"s_kvin{i}") for i in range(2)]
        x_hi, x_lo = sem("x_hi"), sem("x_lo")
        w_hi, w_lo = sem("w_hi"), sem("w_lo")
        v_hi, v_lo = sem("v_hi"), sem("v_lo")
        tab_done = sem("tab_done")
        halves = sem("halves")
        seq_done = sem("seq_done")
        mask_done = sem("mask_done")
        q_done = sem("q_done")
        q_copied = sem("q_copied")
        q_sq = sem("q_sq")
        q_eps = sem("q_eps")
        q_rsd = sem("q_rsd")
        q_mcos, q_msin = sem("q_mcos"), sem("q_msin")
        q_rot = sem("q_rot")
        qt_done = sem("qt_done")
        qt_hi, qt_lo = sem("qt_hi"), sem("qt_lo")
        kvp_done = sem("kvp_done")
        kv_copied = sem("kv_copied")
        k_sq = sem("k_sq")
        k_eps = sem("k_eps")
        k_rsd = sem("k_rsd")
        k_mul = sem("k_mul")
        k_rot = sem("k_rot")
        kt_done = sem("kt_done")
        kt_hi, kt_lo = sem("kt_hi"), sem("kt_lo")
        scored = sem("scored")
        masked = sem("masked")
        biased = sem("biased")
        exped = sem("exped")
        recip = sem("recip")
        normed = sem("normed")
        t_done = sem("t_done")
        pt_hi, pt_lo = sem("pt_hi"), sem("pt_lo")
        pv_done = sem("pv_done")
        o_hi, o_lo = sem("o_hi"), sem("o_lo")
        wo_done = sem("wo_done")
        added = sem("added")
        stored = sem("stored")
        s_w1, s_w2, s_a1, s_b1, s_small = (sem(k) for k in ("s_w1", "s_w2", "s_a1", "s_b1", "s_small"))
        s_ffs = sem("s_ffs")
        w1_hi, w1_lo, w2_hi, w2_lo = sem("w1_hi"), sem("w1_lo"), sem("w2_hi"), sem("w2_lo")
        b1_hi, b1_lo = sem("b1_hi"), sem("b1_lo")
        sm_hi, sm_lo = sem("sm_hi"), sem("sm_lo")
        a1_zero, a1_hi, a1_lo = sem("a1_zero"), sem("a1_hi"), sem("a1_lo")
        lang_done, lbias_done = sem("lang_done"), sem("lbias_done")
        x1_done, x1t_done, x1t_hi, x1t_lo = sem("x1_done"), sem("x1t_done"), sem("x1t_hi"), sem("x1t_lo")
        low_done, low_hi, low_lo = sem("low_done"), sem("low_hi"), sem("low_lo")
        y1_done = sem("y1_done")
        x2_done, x2t_done, x2t_hi, x2t_lo = sem("x2_done"), sem("x2t_done"), sem("x2t_hi"), sem("x2t_lo")
        hl_done = sem("hl_done")
        gates = sem("gates")
        exp_done = sem("exp_done")
        hgt_done, hgt_hi, hgt_lo = sem("hgt_done"), sem("hgt_hi"), sem("hgt_lo")
        y2_done = sem("y2_done")
        top_done, x2_kept, x3_kept = sem("top_done"), sem("x2_kept"), sem("x3_kept")
        GSTEPS = 11
        x3_done, x3t_done, x3t_hi, x3t_lo = sem("x3_done"), sem("x3t_done"), sem("x3t_hi"), sem("x3t_lo")
        s_gu = [sem(f"s_gu{i}") for i in range(2)]
        s_dn = [sem(f"s_dn{i}") for i in range(2)]
        gu_hi, gu_lo = sem("gu_hi"), sem("gu_lo")
        dn_hi, dn_lo = sem("dn_hi"), sem("dn_lo")
        ga_got, ga_hi, ga_lo = sem("ga_got"), sem("ga_hi"), sem("ga_lo")
        db_hi, db_lo = sem("db_hi"), sem("db_lo")
        tg_done, tg_own, tg_hi, tg_lo = sem("tg_done"), sem("tg_own"), sem("tg_hi"), sem("tg_lo")
        g_done, u_done = sem("g_done"), sem("u_done")
        sig_done, gsig_done, act_done = sem("sig_done"), sem("gsig_done"), sem("act_done")
        act_hi, act_lo = sem("act_hi"), sem("act_lo")
        down_done = sem("down_done")
        td_done, td_own, td_hi, td_lo = sem("td_done"), sem("td_own"), sem("td_hi"), sem("td_lo")
        ffn_done, ffn_added = sem("ffn_done"), sem("ffn_added")

        block = ctx.enter_context(nc.Block())

        def product(e, dst, lhs, rhs, first, last):
            e.matmul(dst, lhs(0), rhs(0), start=first, stop=False)
            e.matmul(dst, lhs(0), rhs(1), start=False, stop=False)
            return e.matmul(dst, lhs(1), rhs(0), start=False, stop=last)

        def steps(e, step):
            step(0, 0)
            with e.Fori(0, (NT - PIECES - 2) // 2) as i:
                step(2 * i + 1, 1)
                step(2 * i + 2, 0)
            step(NT - PIECES - 1, 1)
            with e.Fori(0, (PIECES - 2) // 2) as i:
                step(2 * i + NT - PIECES, 0, w=False)
                step(2 * i + NT - PIECES + 1, 1, w=False)
            step(NT - 2, 0, x=False, w=False)
            step(NT - 1, 1, x=False, w=False, nxt=False)

        def tiles(e, half, step):
            odd = (half * FT) % 2
            step(1, 1 - odd)
            step(2, odd)
            with e.Fori(0, (FT - 3) // 2) as i:
                step(2 * i + 3, 1 - odd)
                step(2 * i + 4, odd)

        def settle(e, k):
            e.tensor_tensor(spare[:, k:k + 1], ident[:, 0:1], ident[:, 0:1], ALU.mult)

        @block.sync
        def _(sp):
            def load_x(n, par):
                sp.dma_start(x_raw[:, par, :], t["xT"][ds(n % B), :, :].rearrange("a p n -> p (a n)")).then_inc(s_xin[par], 16)

            def load_w(m, par):
                sp.dma_start(w_raw[:, par, :], t["w_att"][ds(m), :, :].rearrange("a p n -> p (a n)")).then_inc(s_win[par], 16)

            def load_kv(n, par, used=False):
                g, b = n // B, n % B
                _, pages = nc.values_load_multi_w_load_instructions(
                    t["pages"][ds(b), :], engines=[sp.engine], min_val=0, max_val=PAGES - 1,
                    skip_runtime_bounds_check_because="page numbers are below PAGES")
                if used:
                    sp.wait_ge(v_lo, n - 1)
                    sp.wait_ge(kt_done, n - 1)
                for j, page in enumerate(pages):
                    a = PSIZE * (j % 4)
                    sp.dma_start(kv_raw[a:a + PSIZE, par, j // 4, :],
                                 t["kv"][ds(g), ds(page), :, :].rearrange("g a s n -> s (g a n)")).then_inc(s_kvin[par], 16)

            load_x(0, 0)
            load_w(0, 0)
            load_w(1, 1)
            sp.dma_start(ident[:], t["ident"]).then_inc(s_const, 16)
            sp.dma_start(iota[:], t["iota"].partition_broadcast(P)).then_inc(s_const, 16)
            sp.dma_start(seq_i[:], t["seqlens"].partition_broadcast(P)).then_inc(s_const, 16)
            _, lengths = nc.values_load_multi_w_load_instructions(
                t["seqlens"].unsqueeze(0), engines=[sp.engine], min_val=0, max_val=POS_END - 1,
                skip_runtime_bounds_check_because="cache lengths are below POS_END")
            for m in range(2, 4):
                sp.wait_ge(w_lo, m - 1)
                load_w(m, m % 2)
            for b in range(B):
                sp.dma_start(trig[:, b, :], t["trig"][ds(lengths[b], S), :]).then_inc(s_trig, 16)
            sp.dma_start(wnorm, t["wnorm"].partition_broadcast(P)).then_inc(s_trig, 16)
            for m in range(4, PIECES):
                sp.wait_ge(w_lo, m - 1)
                load_w(m, m % 2)
                if m == 5:
                    load_kv(0, 0)
                    load_x(1, 1)
                if m == 6:
                    load_kv(1, 1)
            sp.wait_ge(x_lo, 1)
            load_x(2, 0)
            sp.wait_ge(w_lo, PIECES - 1)
            load_w(PIECES, 0)
            sp.dma_start(acc[:], t["x"].rearrange("b s n -> s b n")).then_inc(s_acc0, 16)

            def step(n, par, x=True, w=True):
                if w:
                    sp.wait_ge(w_lo, n + PIECES)
                    load_w(n + 1 + PIECES, 1 - par)
                if x:
                    sp.wait_ge(x_lo, n + 2)
                    load_x(n + 3, 1 - par)
                load_kv(n + 2, par, True)

            last_w = NT - PIECES - 1
            step(0, 0)
            with sp.Fori(0, (last_w - 1) // 2) as i:
                step(2 * i + 1, 1)
                step(2 * i + 2, 0)
            for n in range(last_w, NT - 2):
                step(n, n % 2, x=n + 3 < NT, w=False)
                if n == NT - PIECES + 1:
                    _, labels = nc.values_load_multi_w_load_instructions(
                        t["label"].unsqueeze(0), engines=[sp.engine], min_val=0, max_val=4,
                        skip_runtime_bounds_check_because="indices of block 1's LoRA are below 5")
                    sp.wait_ge(added, NT - PIECES + 1)
                    sp.dma_start(w1_raw[:], t["w12"][0]).then_inc(s_w1, 16)
                    for b in range(B):
                        sp.dma_start(a1_raw[:, b].rearrange("p c r -> p (c r)"),
                                     t["a1"][ds(labels[b]), :, :].rearrange("a p n -> p (a n)")).then_inc(s_a1, 16)
                    sp.dma_start(w2_raw[:], t["w12"][1]).then_inc(s_w2, 16)

            _, loras = nc.values_load_multi_w_load_instructions(
                t["lora"].unsqueeze(0), engines=[sp.engine], min_val=0, max_val=15,
                skip_runtime_bounds_check_because="indices of the feed-forward's LoRA are below 16")
            sp.wait_ge(added, NT + 1)
            sp.dma_start(b1_raw[0:R1], t["b1"]).then_inc(s_b1, 16)
            sp.dma_start(ra_raw[:].rearrange("p c n -> p (c n)"), t["ra"]).then_inc(s_small, 16)
            sp.dma_start(b2_raw[:], t["b2"]).then_inc(s_small, 16)
            sp.dma_start(lang_i[:], t["lang"].partition_broadcast(P)).then_inc(s_small, 16)
            sp.dma_start(experts[:], t["experts"].partition_broadcast(P)).then_inc(s_small, 16)
            sp.dma_start(lower[:].rearrange("p a b -> p (a b)"), t["lower"].partition_broadcast(P)).then_inc(s_small, 16)
            sp.dma_start(own_rows[:], t["own"]).then_inc(s_small, 16)
            for b in range(B):
                rows = slice(b * R3, (b + 1) * R3)
                for k in range(2):
                    sp.dma_start(gu_a[:, k, b, :], t["gu_a"][k, ds(loras[b]), :, :].rearrange("a p n -> p (a n)")).then_inc(s_ffs, 16)
                    sp.dma_start(gu_b[rows, k, :], t["gu_b"][k, ds(loras[b]), :, :].rearrange("a r n -> r (a n)")).then_inc(s_ffs, 16)
                sp.dma_start(d_a[:, :, rows], t["d_a"][ds(loras[b]), :, :, :].rearrange("a p f r -> p (a f) r")).then_inc(s_ffs, 16)
                sp.dma_start(d_b[rows, :], t["d_b"][ds(loras[b]), :, :].rearrange("a r n -> r (a n)")).then_inc(s_ffs, 16)
            sp.wait_ge(s_ffs, 16 * 6 * B)
            def load_fw(m, ft, par):
                raw = fw_raw[par]

                def load(lo, hi, src, done):
                    sp.dma_start(raw[:, lo:hi], t["fw"][src, ds(ft), :, :].rearrange("a p n -> p (a n)")).then_inc(done, 16)

                if not (isinstance(m, int) and m < 2):
                    sp.wait_ge(gu_lo, m - 1)
                load(F_GATE, F_GATE_B, 0, s_gu[par])
                load(F_UP, F_UP_B, 1, s_gu[par])
                sp.dma_start(raw[:, F_GATE_B:F_GATE_B + P], gu_b[:, 0, ds(ft * P, P)]).then_inc(s_gu[par], 16)
                sp.dma_start(raw[:, F_UP_B:F_UP_B + P], gu_b[:, 1, ds(ft * P, P)]).then_inc(s_gu[par], 16)
                if not (isinstance(m, int) and m < 2):
                    sp.wait_ge(dn_lo, m - 1)
                load(F_DOWN, F_DOWN_A, 2, s_dn[par])
                sp.dma_start(raw[:, F_DOWN_A:FW], d_a[:, ds(ft), :].rearrange("p f n -> p (f n)")).then_inc(s_dn[par], 16)

            sp.wait_ge(w2_lo, 1)
            load_fw(0, 0, 0)
            for half in range(2):
                if half:
                    load_fw(FT, 0, FT % 2)
                tiles(sp, half, lambda ft, par: load_fw(half * FT + ft, ft, par))
            for b in range(B):
                sp.wait_ge(ffn_added, b + 1)
                sp.dma_start(out[b], acc[:, b, :]).then_inc(stored, 16)
            sp.wait_ge(stored, 16 * B)

        @block.gpsimd
        def _(pool):
            def x_low(n, par):
                pool.wait_ge(x_hi, n + 1)
                pool.tensor_tensor(x_pair[par][:, 1], x_raw[:, par, :].rearrange("p (c n) -> p c n", c=DC),
                                   x_pair[par][:, 0].bitcast(F32), ALU.subtract).then_inc(x_lo, 1)

            def w_low(m, par):
                at = (m % (2 * PIECES)) * PW
                pool.wait_ge(w_hi, m + 1)
                pool.tensor_tensor(w_pair[:, 1, ds(at, PW)], w_raw[:, par, :],
                                   w_pair[:, 0, ds(at, PW)].bitcast(F32), ALU.subtract).then_inc(w_lo, 1)

            def v_low(n, par):
                pool.wait_ge(v_hi, n + 1)
                pool.tensor_tensor(v_pair[par][:, 1], kv_raw[:, par, :, D:2 * D],
                                   v_pair[par][:, 0].bitcast(F32), ALU.subtract).then_inc(v_lo, 1)

            def q_norm(n, par):
                pool.wait_ge(q_sq, n + 1)
                settle(pool, 0)
                pool.tensor_scalar(q_se[:], q_ss[:], D * EPS, None, ALU.add).then_inc(q_eps, 1)
                pool.wait_ge(q_eps, n + 1)
                pool.tensor_tensor(q_rs[par][:], q_se[:], half_neg[:], ALU.pow).then_inc(q_rsd, 1)

            def k_norm(n):
                pool.wait_ge(k_sq, n + 1)
                settle(pool, 1)
                pool.tensor_scalar(k_se[:], k_ss[:], D * EPS, None, ALU.add).then_inc(k_eps, 1)
                pool.wait_ge(k_eps, n + 1)
                pool.tensor_tensor(k_rs[:], k_se[:], half_neg[:, 0:1], ALU.pow).then_inc(k_rsd, 1)

            def q_rotate(n):
                pool.wait_ge(q_copied, n + 1)
                if isinstance(n, int) and n == 0:
                    pool.wait_ge(tab_done, 1)
                else:
                    pool.wait_ge(q_rot, n)
                pool.tensor_tensor(q_sin[:], q_sb[:], tabs[:, ds(n % B), 1, :].broadcast_to([P, REP, D]),
                                   ALU.mult).then_inc(q_msin, 1)
                pool.wait_ge(q_mcos, n + 1)
                pool.wait_ge(q_msin, n + 1)
                h = D // 2
                pool.tensor_tensor(q_cos[:, :, 0:h], q_cos[:, :, 0:h], q_sin[:, :, h:D], ALU.add)
                pool.tensor_tensor(q_cos[:, :, h:D], q_cos[:, :, h:D], q_sin[:, :, 0:h], ALU.add).then_inc(q_rot, 1)

            pool.memset(spare[:, 2:3], 0.0).then_inc(added, 1)
            pool.memset(mask[:, :, CACHE:KEYS], 0.0)
            pool.memset(half_neg[:], -0.5).then_inc(halves, 1)
            x_low(0, 0)
            for m in range(QKV_PIECES + 1):
                w_low(m, m % 2)
            pool.wait_ge(halves, 1)
            k_norm(0)
            q_rotate(0)
            q_norm(0, 0)
            x_low(1, 1)
            w_low(PIECES - 2, 0)

            def step(n, par, x=True, w=True, nxt=True):
                if nxt:
                    k_norm(n + 1)
                    q_rotate(n + 1)
                    q_norm(n + 1, 1 - par)
                v_low(n, par)
                if isinstance(n, int) and n == 0:
                    w_low(PIECES - 1, 1)
                if x:
                    x_low(n + 2, par)
                if w:
                    w_low(n + PIECES, par)

            steps(pool, step)

            pool.wait_ge(added, NT - PIECES + 1)
            pool.memset(a1_pair[:].rearrange("p k c n -> p (k c n)").bitcast(F32), 0.0).then_inc(a1_zero, 1)

            def a1_low(b):
                pool.wait_ge(a1_hi, b + 1)
                pool.tensor_tensor(a1_pair[:, 1, :, 0:R1], a1_raw[:, ds(b), :, :].rearrange("p b c r -> p (b c) r"),
                                   a1_pair[:, 0, :, 0:R1].bitcast(F32), ALU.subtract).then_inc(a1_lo, 1)

            a1_low(0)
            with pool.Fori(1, B) as b:
                a1_low(b)

            def fw_low(m, par, cols, hi_sem, lo_sem):
                pool.wait_ge(hi_sem, m + 1)
                pool.tensor_tensor(fw_pair[par][:, 1, cols], fw_raw[par][:, cols], fw_pair[par][:, 0, cols].bitcast(F32),
                                   ALU.subtract).then_inc(lo_sem, 1)

            def ff_step(m, par):
                fw_low(m, par, GU, gu_hi, gu_lo)
                fw_low(m - 1, 1 - par, DN, dn_hi, dn_lo)

            fw_low(0, 0, GU, gu_hi, gu_lo)
            for half in range(2):
                if half:
                    ff_step(FT, FT % 2)
                tiles(pool, half, lambda ft, par: ff_step(half * FT + ft, par))
            fw_low(2 * FT - 1, 1, DN, dn_hi, dn_lo)

        @block.scalar
        def _(act):
            def copy_q(n):
                act.wait_ge(q_done, n + 1)
                if not (isinstance(n, int) and n == 0):
                    act.wait_ge(q_mcos, n)
                    act.wait_ge(q_msin, n)
                act.activation(q_sb[:].rearrange("p h d -> p (h d)"), q_ps, ACT.Copy).then_inc(q_copied, 1)

            def square_q(n):
                act.wait_ge(q_copied, n + 1)
                for h in range(REP):
                    last = act.activation(q_ps[:, h * D:(h + 1) * D], q_sb[:, h, :], ACT.Square, accum_out=q_ss[:, h:h + 1])
                last.then_inc(q_sq, 1)

            def copy_kv(n, par):
                act.wait_ge(kvp_done, n + 1)
                if not (isinstance(n, int) and n < 2):
                    act.wait_ge(v_lo, n - 1)
                    act.wait_ge(kt_done, n - 1)
                act.activation(kv_raw[:, par, KC - 1, :], misc_ps[:, 0:2 * D], ACT.Copy).then_inc(kv_copied, 1)
                act.wait_ge(kv_copied, n + 1)
                act.activation(squares[:], kv_raw[:, par, KC - 1, 0:D], ACT.Square, accum_out=k_ss[:]).then_inc(k_sq, 1)

            def x_high(n, par):
                act.wait_ge(s_xin[par], 16 * (n // 2 + 1))
                if not (isinstance(n, int) and n < 2):
                    act.wait_ge(q_done, n - 1)
                act.activation(x_pair[par][:, 0], x_raw[:, par, :].rearrange("p (c n) -> p c n", c=DC),
                               ACT.Copy).then_inc(x_hi, 1)

            def v_high(n, par):
                act.wait_ge(s_kvin[par], 16 * NPP * (n // 2 + 1))
                if not (isinstance(n, int) and n < 2):
                    act.wait_ge(pv_done, n - 1)
                act.activation(v_pair[par][:, 0], kv_raw[:, par, :, D:2 * D], ACT.Copy).then_inc(v_hi, 1)

            def qt_high(n):
                act.wait_ge(qt_done, n + 1)
                act.activation(qt_pair[:, 0].rearrange("p h n -> p (h n)"), q_ps, ACT.Copy).then_inc(qt_hi, 1)

            def kt_high(n):
                act.wait_ge(kt_done, n + 1)
                act.activation(kt_pair[:, 0], kt_ps, ACT.Copy).then_inc(kt_hi, 1)

            def o_high(n):
                act.wait_ge(pv_done, n + 1)
                act.activation(o_pair[:, 0].rearrange("p h n -> p (h n)"), misc_ps, ACT.Copy).then_inc(o_hi, 1)

            def pt_high(n, h):
                act.wait_ge(t_done, REP * n + h + 1)
                act.activation(pt_pair[:, 0, h].rearrange("p c n -> p (c n)"), pt_ps, ACT.Copy).then_inc(pt_hi, 1)

            def exponent(n, par, h):
                act.wait_ge(biased, REP * n + h + 1)
                act.wait_ge(q_rsd, n + 1)
                act.activation(prob[:, h, :], prob[:, h, :], ACT.Exp, bias=nbias[:, h:h + 1],
                               scale=q_rs[par][:, h:h + 1], accum_out=psum_row[:, h:h + 1]).then_inc(exped, 1)

            def step(n, par, x=True, w=True, nxt=True):
                first = isinstance(n, int) and n == 0
                exponent(n, par, 0)
                exponent(n, par, 1)
                if not first:
                    pt_high(n - 1, 3)
                if nxt:
                    copy_kv(n + 1, 1 - par)
                    copy_q(n + 1)
                    square_q(n + 1)
                v_high(n, par)
                exponent(n, par, 2)
                if not first:
                    o_high(n - 1)
                pt_high(n, 0)
                if nxt:
                    qt_high(n + 1)
                    kt_high(n + 1)
                pt_high(n, 1)
                exponent(n, par, 3)
                if x:
                    x_high(n + 2, par)
                pt_high(n, 2)

            x_high(0, 0)
            copy_kv(0, 0)
            copy_q(0)
            square_q(0)
            x_high(1, 1)
            qt_high(0)
            kt_high(0)
            steps(act, step)
            pt_high(NT - 1, 3)
            act.wait_ge(s_w1, 16)
            act.activation(w1_pair[:, 0].rearrange("p c n -> p (c n)"), w1_raw[:], ACT.Copy).then_inc(w1_hi, 1)
            o_high(NT - 1)

            def to_high(dst, src, done, count, hi_sem, scale=1.0):
                act.wait_ge(done, count)
                act.activation(dst, src, ACT.Copy, scale=scale).then_inc(hi_sem, 1)

            def x1t_high(b):
                to_high(x1t_pair[:, 0].rearrange("p c n -> p (c n)"), banks[:, 0, :], x1t_done, b + 1, x1t_hi)

            def x2t_high(b):
                to_high(x2t_pair[:, 0].rearrange("p c n -> p (c n)"), banks[:, 3, :], x2t_done, b + 1, x2t_hi)

            def low_high(b):
                to_high(low_pair[:, 0], banks[0:R1, 1, 0:P], low_done, b + 1, low_hi, LORA1_SCALE)

            def keep(x_sb, b, done, kept):
                to_high(acc[:, ds(b), :].rearrange("p b n -> p (b n)"), x_sb[:], done, b + 1, kept)

            def stage(b, nxt=True, after=True):
                act.wait_ge(gates, GSTEPS * b + 2)
                act.activation(expl[:], logits[:], ACT.Exp).then_inc(exp_done, 1)
                if nxt:
                    low_high(b + 1)
                    keep(x2_sb, b + 1, x2_done, x2_kept)
                to_high(hgt_pair[:, 0], banks[:, 5, 0:P], hgt_done, b + 1, hgt_hi)
                if nxt:
                    x2t_high(b + 1)
                else:
                    lora_high(tg_pair[0], tg_own, 1, tg_hi)
                if after:
                    x1t_high(b + 2)
                keep(x3_sb, b, x3_done, x3_kept)
                to_high(x3t_pair[:, 0, :, ds(b * S, S)], banks[:, 7, :].rearrange("p (c n) -> p c n", c=DC),
                        x3t_done, b + 1, x3t_hi)

            x1t_high(0)
            to_high(b1_pair[:, 0], b1_raw[0:R1], s_b1, 16, b1_hi)
            low_high(0)
            act.wait_ge(s_small, 16 * 6)
            act.activation(ra_pair[:, 0], ra_raw[:], ACT.Copy)
            act.activation(b2_pair[:, 0], b2_raw[:], ACT.Copy).then_inc(sm_hi, 1)
            to_high(w2_pair[:, 0].rearrange("p c n -> p (c n)"), w2_raw[:], s_w2, 16, w2_hi)
            keep(x2_sb, 0, x2_done, x2_kept)
            x2t_high(0)
            x1t_high(1)
            def lora_high(pair, done, n, hi_sem):
                to_high(pair[:, 0], own_f[:].rearrange("p b n -> p (b n)"), done, n, hi_sem)

            def gu_high(m, par):
                act.wait_ge(s_gu[par], 16 * 4 * (m // 2 + 1))
                if not (isinstance(m, int) and m < 2):
                    act.wait_ge(u_done, m - 1)
                act.activation(fw_pair[par][:, 0, GU], fw_raw[par][:, GU], ACT.Copy).then_inc(gu_hi, 1)

            with act.Fori(0, B - 2) as b:
                stage(b)
            for k in range(2):
                to_high(ga_pair[k][:, 0], ga_f[:, k], ga_got, k + 1, ga_hi)
            gu_high(0, 0)
            stage(B - 2, after=False)
            stage(B - 1, nxt=False, after=False)

            act.wait_ge(x3t_lo, B)
            act.wait_ge(s_ffs, 16 * 6 * B)
            act.activation(db_pair[:, 0], d_b[:], ACT.Copy).then_inc(db_hi, 1)
            def dn_high(m, par):
                act.wait_ge(s_dn[par], 16 * 2 * (m // 2 + 1))
                if not (isinstance(m, int) and m < 2):
                    act.wait_ge(down_done, m - 1)
                act.activation(fw_pair[par][:, 0, DN], fw_raw[par][:, DN], ACT.Copy).then_inc(dn_hi, 1)

            def swish(m, par):
                act.wait_ge(g_done, m + 1)
                act.activation(sig[:], g_ps, ACT.Sigmoid).then_inc(sig_done, 1)
                to_high(act_pair[par][:, 0], act_f[:], act_done, m + 1, act_hi)

            def ff_step(m, par):
                gu_high(m, par)
                dn_high(m - 1, 1 - par)
                swish(m - 1, 1 - par)

            lora_high(tg_pair[1], tg_own, 2, tg_hi)
            tiles(act, 0, ff_step)
            ff_step(FT, FT % 2)
            lora_high(tg_pair[0], tg_own, 3, tg_hi)
            lora_high(td_pair, td_own, 1, td_hi)
            lora_high(tg_pair[1], tg_own, 4, tg_hi)
            tiles(act, 1, lambda ft, par: ff_step(FT + ft, par))
            dn_high(2 * FT - 1, 1)
            swish(2 * FT - 1, 1)
            lora_high(td_pair, td_own, 2, td_hi)

        @block.vector
        def _(dve):
            def q_times_cos(n):
                dve.wait_ge(q_copied, n + 1)
                if not (isinstance(n, int) and n == 0):
                    dve.wait_ge(qt_done, n)
                dve.tensor_tensor(q_cos[:], q_sb[:], tabs[:, ds(n % B), 0, :].broadcast_to([P, REP, D]),
                                  ALU.mult).then_inc(q_mcos, 1)

            def k_rope(n, par):
                dve.wait_ge(k_rsd, n + 1)
                for k, dst in enumerate((k_cos, k_sin)):
                    dve.scalar_tensor_tensor(out=dst[:], in0=kv_raw[:, par, KC - 1, 0:D], scalar=k_rs[:, 0:1],
                                             in1=tabs[:, ds(n % B), 2 + k, :].rearrange("p a d -> p (a d)"),
                                             op0=ALU.mult, op1=ALU.mult).then_inc(k_mul, 1)
                dve.wait_ge(k_mul, 2 * n + 2)
                h = D // 2
                dst = kv_raw[:, par, KC - 1, 0:D]
                dve.tensor_tensor(dst[:, 0:h], k_cos[:, 0:h], k_sin[:, h:D], ALU.add)
                dve.tensor_tensor(dst[:, h:D], k_cos[:, h:D], k_sin[:, 0:h], ALU.add).then_inc(k_rot, 1)

            def low(hi_sem, count, pair, src, lo_sem):
                dve.wait_ge(hi_sem, count)
                dve.tensor_tensor(pair[1], src, pair[0].bitcast(F32), ALU.subtract).then_inc(lo_sem, 1)

            def qt_low(n):
                low(qt_hi, n + 1, [qt_pair[:, k].rearrange("p h n -> p (h n)") for k in range(2)], q_ps, qt_lo)

            def kt_low(n):
                low(kt_hi, n + 1, [kt_pair[:, k] for k in range(2)], kt_ps, kt_lo)

            def o_low(n):
                low(o_hi, n + 1, [o_pair[:, k].rearrange("p h n -> p (h n)") for k in range(2)], misc_ps, o_lo)

            def pt_low(n, h):
                low(pt_hi, REP * n + h + 1, [pt_pair[:, k, h].rearrange("p c n -> p (c n)") for k in range(2)],
                    pt_ps, pt_lo)

            def mask_max(n, par, h):
                dve.wait_ge(scored, REP * n + h + 1)
                if h == 0:
                    dve.wait_ge(mask_done, n + 1)
                if not (isinstance(n, int) and n == 0):
                    dve.wait_ge(t_done, REP * (n - 1) + h + 1)
                settle(dve, 12 + h)
                two = prob[:, h, :].rearrange("p (a n) -> p a n", a=2)
                dve.tensor_tensor_reduce(out=two, in0=score_ps[h % 2][:, :, 0:HALF],
                                         in1=mask[:, par, :].rearrange("p (a n) -> p a n", a=2),
                                         scale=1.0, scalar=-3e38, op0=ALU.add, op1=ALU.max,
                                         accum_out=smax[:, h:h + 1]).then_inc(masked, 1)
                dve.wait_ge(masked, REP * n + h + 1)
                dve.wait_ge(q_rsd, n + 1)
                dve.tensor_scalar(nbias[:, h:h + 1], smax[:, h:h + 1], q_rs[par][:, h:h + 1], -1.0,
                                  ALU.mult, ALU.mult).then_inc(biased, 1)

            def normalise(n, h):
                dve.wait_ge(exped, REP * n + h + 1)
                dve.reciprocal(rsum[:, h:h + 1], psum_row[:, h:h + 1]).then_inc(recip, 1)
                dve.wait_ge(recip, REP * n + h + 1)
                dve.tensor_scalar(prob[:, h, :], prob[:, h, :], rsum[:, h:h + 1], None,
                                  ALU.mult).then_inc(normed, 1)

            def make_mask(n, par):
                if not (isinstance(n, int) and n < 2):
                    dve.wait_ge(masked, REP * (n - 1))
                dve.tensor_scalar(mask[:, par, 0:CACHE], iota[:], seq_f[:, ds(n % B)], NEG, ALU.is_ge,
                                  ALU.mult).then_inc(mask_done, 1)

            def w_high(m, par):
                dve.wait_ge(s_win[par], 16 * (m // 2 + 1))
                if not (isinstance(m, int) and m < PIECES):
                    dve.wait_ge(kvp_done, m - PIECES + 1)
                dve.tensor_scalar(w_pair[:, 0, ds((m % (2 * PIECES)) * PW, PW)], w_raw[:, par, :], 1.0, None,
                                  ALU.mult).then_inc(w_hi, 1)

            def add_attention(n):
                dve.wait_ge(wo_done, n + 1)
                dst = acc[:, ds(n % B), :].rearrange("p a n -> p (a n)")
                dve.tensor_tensor(dst, misc_ps, dst, ALU.add).then_inc(added, 1)

            for m in range(QKV_PIECES):
                w_high(m, m % 2)
            dve.wait_ge(s_trig, 16 * (B + 1))
            h = D // 2
            cos, sin = trig[:, :, 0:h], trig[:, :, h:D]
            for k in range(2):
                scale = 1.0 if k == 0 else float(D) ** 0.5
                for j, (src, sign, tab) in enumerate(((cos, 1, 0), (cos, 1, 0), (sin, 1, 1), (sin, -1, 1))):
                    half = slice(h * (j % 2), h * (j % 2) + h)
                    last = dve.scalar_tensor_tensor(
                        out=tabs[:, :, 2 * k + tab, half], in0=src, scalar=sign * scale,
                        in1=wnorm[:, k, half].unsqueeze(1).broadcast_to([P, B, h]), op0=ALU.mult, op1=ALU.mult)
            last.then_inc(tab_done, 1)
            w_high(QKV_PIECES, QKV_PIECES % 2)
            dve.wait_ge(s_const, 48)
            dve.tensor_copy(seq_f[:], seq_i[:]).then_inc(seq_done, 1)
            dve.wait_ge(seq_done, 1)
            dve.wait_ge(halves, 1)
            make_mask(0, 0)
            dve.wait_ge(tab_done, 1)
            k_rope(0, 0)
            q_times_cos(0)
            qt_low(0)
            kt_low(0)
            w_high(PIECES - 2, 0)

            def step(n, par, x=True, w=True, nxt=True):
                first = isinstance(n, int) and n == 0
                mask_max(n, par, 0)
                mask_max(n, par, 1)
                normalise(n, 0)
                if not first:
                    pt_low(n - 1, 3)
                normalise(n, 1)
                if nxt:
                    make_mask(n + 1, 1 - par)
                mask_max(n, par, 2)
                if nxt:
                    q_times_cos(n + 1)
                    k_rope(n + 1, 1 - par)
                normalise(n, 2)
                if first:
                    w_high(PIECES - 1, 1)
                if w:
                    w_high(n + PIECES, par)
                if not first:
                    o_low(n - 1)
                pt_low(n, 0)
                mask_max(n, par, 3)
                if nxt:
                    qt_low(n + 1)
                pt_low(n, 1)
                if nxt:
                    kt_low(n + 1)
                normalise(n, 3)
                pt_low(n, 2)
                if not first:
                    add_attention(n - 1)
                if first:
                    dve.wait_ge(s_acc0, 16)

            def flat(ap):
                return ap.rearrange("p c n -> p (c n)")

            steps(dve, step)
            pt_low(NT - 1, 3)
            low(w1_hi, 1, [flat(w1_pair[:, k]) for k in range(2)], w1_raw[:], w1_lo)
            o_low(NT - 1)
            add_attention(NT - 1)

            def begin_a(b):
                if isinstance(b, int) and b == 0:
                    dve.wait_ge(s_a1, 16 * B)
                    dve.wait_ge(a1_zero, 1)
                else:
                    dve.wait_ge(low_done, b)
                    dve.wait_ge(x2_done, b)
                dve.tensor_scalar(a1_pair[:, 0, :, 0:R1], a1_raw[:, ds(b), :, :].rearrange("p b c r -> p (b c) r"),
                                  1.0, None, ALU.mult).then_inc(a1_hi, 1)
                dve.tensor_scalar(x1_sb[:], acc[:, ds(b), :].rearrange("p b n -> p (b n)"), 1.0, None,
                                  ALU.mult).then_inc(x1_done, 1)

            def x1t_low(b):
                low(x1t_hi, b + 1, [flat(x1t_pair[:, k]) for k in range(2)], banks[:, 0, :], x1t_lo)

            def lora1_low(b):
                dve.wait_ge(low_hi, b + 1)
                dve.scalar_tensor_tensor(out=low_pair[:, 1], in0=banks[0:R1, 1, 0:P], scalar=LORA1_SCALE,
                                         in1=low_pair[:, 0].bitcast(F32), op0=ALU.mult,
                                         op1=ALU.subtract).then_inc(low_lo, 1)

            def end_a(b):
                dve.wait_ge(y1_done, b + 1)
                if not (isinstance(b, int) and b == 0):
                    dve.wait_ge(x2_kept, b)
                dve.tensor_tensor(x2_sb[:], banks[:, 2, :], x1_sb[:], ALU.add).then_inc(x2_done, 1)

            def gate_start(b):
                n = GSTEPS * b
                dve.wait_ge(hl_done, b + 1)
                dve.tensor_tensor(logits[:], banks[:, 4, 0:E], lbias[:, ds(b), :].rearrange("p b e -> p (b e)"),
                                  ALU.add).then_inc(gates, 1)
                dve.wait_ge(gates, n + 1)
                dve.tensor_reduce(top[:], logits[:], mybir.AxisListType.X, ALU.max).then_inc(top_done, 1)
                dve.wait_ge(top_done, b + 1)
                dve.tensor_scalar(logits[:], logits[:], top[:], None, ALU.subtract).then_inc(gates, 1)

            def gate_end(b):
                n = GSTEPS * b
                every = logits[:].unsqueeze(1).broadcast_to([P, E, E])
                own = logits[:].unsqueeze(2).broadcast_to([P, E, E])
                dve.wait_ge(gates, n + 2)
                dve.tensor_tensor(above[:], every, own, ALU.is_gt)
                dve.tensor_tensor(equal[:], every, own, ALU.is_equal).then_inc(gates, 1)
                dve.wait_ge(gates, n + 3)
                dve.tensor_tensor(equal[:], equal[:], lower[:], ALU.mult).then_inc(gates, 1)
                dve.wait_ge(gates, n + 4)
                dve.tensor_tensor(above[:], above[:], equal[:], ALU.add).then_inc(gates, 1)
                dve.wait_ge(gates, n + 5)
                dve.tensor_reduce(rank[:], above[:], mybir.AxisListType.X, ALU.add).then_inc(gates, 1)
                dve.wait_ge(gates, n + 6)
                dve.wait_ge(exp_done, b + 1)
                dve.scalar_tensor_tensor(out=gate[:], in0=rank[:], scalar=1.5, in1=expl[:], op0=ALU.is_lt,
                                         op1=ALU.mult).then_inc(gates, 1)
                dve.wait_ge(gates, n + 7)
                dve.tensor_reduce(gsum[:], gate[:], mybir.AxisListType.X, ALU.add).then_inc(gates, 1)
                dve.wait_ge(gates, n + 8)
                dve.reciprocal(grec[:], gsum[:]).then_inc(gates, 1)
                dve.wait_ge(gates, n + 9)
                dve.tensor_scalar(gate[:], gate[:], grec[:], LORA2_SCALE, ALU.mult, ALU.mult).then_inc(gates, 1)
                dve.wait_ge(gates, n + 10)
                dve.tensor_tensor(hg[:], banks[:, 4, E:E + ER].rearrange("p (e r) -> p e r", e=E),
                                  gate[:].unsqueeze(2).broadcast_to([P, E, R2]), ALU.mult).then_inc(gates, 1)

            def end_b(b):
                dve.wait_ge(y2_done, b + 1)
                dve.wait_ge(x2_kept, b + 1)
                if not (isinstance(b, int) and b == 0):
                    dve.wait_ge(x3_kept, b)
                dve.tensor_tensor(x3_sb[:], banks[:, 6, :], acc[:, ds(b), :].rearrange("p b n -> p (b n)"),
                                  ALU.add).then_inc(x3_done, 1)

            def x2t_low(b):
                low(x2t_hi, b + 1, [flat(x2t_pair[:, k]) for k in range(2)], banks[:, 3, :], x2t_lo)

            def stage(b, nxt=True, after=True):
                gate_start(b)
                gate_end(b)
                if nxt:
                    lora1_low(b + 1)
                    end_a(b + 1)
                low(hgt_hi, b + 1, [hgt_pair[:, k] for k in range(2)], banks[:, 5, 0:P], hgt_lo)
                if not nxt:
                    gate_up_lora(0, banks[:, 0, :])
                if after:
                    begin_a(b + 2)
                end_b(b)
                if nxt:
                    x2t_low(b + 1)
                if after:
                    x1t_low(b + 2)
                low(x3t_hi, b + 1, [x3t_pair[:, k, :, ds(b * S, S)] for k in range(2)],
                    banks[:, 7, :].rearrange("p (c n) -> p c n", c=DC), x3t_lo)

            def own(src, half):
                return dve.tensor_tensor(own_f[:], src.rearrange("p (b n) -> p b n", b=HB),
                                         own_rows[:, half * HB:(half + 1) * HB].unsqueeze(2).broadcast_to([P, HB, S]),
                                         ALU.mult)

            def gate_up_lora(n, bank=tg_ps, used=None):
                dve.wait_ge(tg_done, n + 1)
                if used:
                    dve.wait_ge(*used)
                own(bank, n // 2).then_inc(tg_own, 1)
                low(tg_hi, n + 1, [tg_pair[n % 2][:, j] for j in range(2)], own_f[:].rearrange("p b n -> p (b n)"), tg_lo)

            begin_a(0)
            x1t_low(0)
            low(b1_hi, 1, [b1_pair[:, k] for k in range(2)], b1_raw[0:R1], b1_lo)
            lora1_low(0)
            dve.wait_ge(sm_hi, 1)
            dve.tensor_tensor(ra_pair[:, 1], ra_raw[:], ra_pair[:, 0].bitcast(F32), ALU.subtract)
            dve.tensor_tensor(b2_pair[:, 1], b2_raw[:], b2_pair[:, 0].bitcast(F32), ALU.subtract).then_inc(sm_lo, 1)
            end_a(0)
            begin_a(1)
            x2t_low(0)
            x1t_low(1)
            dve.tensor_copy(lang_f[:], lang_i[:]).then_inc(lang_done, 1)
            dve.wait_ge(lang_done, 1)
            for b in range(B):
                last = dve.tensor_scalar(lbias[:, b, :], experts[:], lang_f[:, b:b + 1], LANG_BIAS,
                                         ALU.is_equal, ALU.mult)
            last.then_inc(lbias_done, 1)
            low(w2_hi, 1, [flat(w2_pair[:, k]) for k in range(2)], w2_raw[:], w2_lo)
            dve.wait_ge(lbias_done, 1)
            with dve.Fori(0, B - 2) as b:
                stage(b)
            dve.wait_ge(s_ffs, 16 * 6 * B)
            for k in range(2):
                for c in range(DC):
                    last = dve.tensor_copy(ga_f[:, k, c].rearrange("p (b r) -> p b r", b=B),
                                           gu_a[:, k, :, c * R3:(c + 1) * R3])
                last.then_inc(ga_got, 1)
            for k in range(2):
                low(ga_hi, k + 1, [ga_pair[k][:, j] for j in range(2)], ga_f[:, k], ga_lo)
            stage(B - 2, after=False)
            stage(B - 1, nxt=False, after=False)

            def gated(m, par):
                dve.wait_ge(sig_done, m + 1)
                dve.tensor_tensor(gsig[:], g_ps, sig[:], ALU.mult).then_inc(gsig_done, 1)
                dve.wait_ge(gsig_done, m + 1)
                dve.wait_ge(u_done, m + 1)
                if not (isinstance(m, int) and m == 0):
                    dve.wait_ge(act_lo, m)
                dve.tensor_tensor(act_f[:], u_ps, gsig[:], ALU.mult).then_inc(act_done, 1)
                low(act_hi, m + 1, [act_pair[par][:, k] for k in range(2)], act_f[:], act_lo)

            def down_lora(half, used):
                dve.wait_ge(td_done, half + 1)
                dve.wait_ge(*used)
                own(t_ps, half).then_inc(td_own, 1)
                low(td_hi, half + 1, [td_pair[:, j] for j in range(2)], own_f[:].rearrange("p b n -> p (b n)"), td_lo)

            def add_ffn(half):
                for b in range(half * HB, (half + 1) * HB):
                    dve.wait_ge(ffn_done, b + 1)
                    dve.tensor_tensor(acc[:, b, :], ffn_bank[b % HB], acc[:, b, :], ALU.add).then_inc(ffn_added, 1)

            gate_up_lora(1, banks[:, 1, :], (tg_lo, 1))
            low(db_hi, 1, [db_pair[:, k] for k in range(2)], d_b[:], db_lo)
            gated(0, 0)
            tiles(dve, 0, gated)
            gate_up_lora(2, used=(tg_lo, 2))
            down_lora(0, (tg_lo, 3))
            gate_up_lora(3, used=(td_lo, 1))
            gated(FT, FT % 2)
            add_ffn(0)
            tiles(dve, 1, lambda ft, par: gated(FT + ft, par))
            down_lora(1, (tg_lo, 4))
            add_ffn(1)

        @block.tensor
        def _(pe):
            def group_at(n):
                return ((n // B) % 2) * GW

            def project_q(n, par):
                if not (isinstance(n, int) and n == 0):
                    pe.wait_ge(qt_lo, n)
                at = group_at(n)
                for c in range(DC):
                    last = product(pe, q_ps, lambda k: x_pair[par][:, k, c, :],
                                   lambda k: w_pair[:, k, ds(at + c * REP * P, REP * P)], c == 0, c == DC - 1)
                last.then_inc(q_done, 1)

            def project_kv(n, par):
                pe.wait_ge(x_lo, n + 1)
                pe.wait_ge(w_lo, (n // B) * PIECES + QKV_PIECES)
                if isinstance(n, int) and n == 1:
                    pe.wait_ge(kv_copied, 1)
                elif not (isinstance(n, int) and n == 0):
                    pe.wait_ge(added, n - 1)
                at = group_at(n) + WKV
                for c in range(DC):
                    last = product(pe, misc_ps[:, 0:2 * D], lambda k: x_pair[par][:, k, c, :],
                                   lambda k: w_pair[:, k, ds(at + c * 2 * D, 2 * D)], c == 0, c == DC - 1)
                last.then_inc(kvp_done, 1)

            def transpose_q(n):
                pe.wait_ge(q_rot, n + 1)
                pe.wait_ge(q_sq, n + 1)
                for h in range(REP):
                    last = pe.transpose(q_ps[:, h * P:(h + 1) * P], q_cos[:, h, :], ident[:])
                last.then_inc(qt_done, 1)

            def transpose_cached_k(n, par):
                pe.wait_ge(s_kvin[par], 16 * NPP * (n // 2 + 1))
                if not (isinstance(n, int) and n == 0):
                    pe.wait_ge(masked, REP * (n - 1) + 3)
                for c in range(KC - 1):
                    pe.transpose(kt_ps[:, c * P:(c + 1) * P], kv_raw[:, par, c, 0:D], ident[:])

            def transpose_new_k(n, par):
                pe.wait_ge(k_rot, n + 1)
                pe.transpose(kt_ps[:, CACHE:KEYS], kv_raw[:, par, KC - 1, 0:D], ident[:]).then_inc(kt_done, 1)

            def scores(n, h):
                if h == 0:
                    pe.wait_ge(qt_lo, n + 1)
                    pe.wait_ge(kt_lo, n + 1)
                elif h > 1:
                    pe.wait_ge(masked, REP * n + h - 1)
                elif not (isinstance(n, int) and n == 0):
                    pe.wait_ge(masked, REP * n)
                for a in range(2):
                    last = product(pe, score_ps[h % 2][:, a, 0:HALF], lambda k: qt_pair[:, k, h, :],
                                   lambda k: kt_pair[:, k, a * HALF:(a + 1) * HALF], True, True)
                last.then_inc(scored, 1)

            def transpose_p(n, h):
                pe.wait_ge(normed, REP * n + h + 1)
                if not (isinstance(n, int) and n == 0 and h == 0):
                    pe.wait_ge(pt_lo, REP * n + h)
                for c in range(KC):
                    last = pe.transpose(pt_ps[:, c * P:(c + 1) * P], prob[:, h, c * P:(c + 1) * P], ident[:])
                last.then_inc(t_done, 1)

            def values(n, par, steady=True):
                pe.wait_ge(pt_lo, REP * (n + 1))
                pe.wait_ge(v_lo, n + 1)
                if steady:
                    pe.wait_ge(kv_copied, n + 3)
                for c in range(KC):
                    last = product(pe, misc_ps.rearrange("p (h n) -> p h n", h=REP),
                                   lambda k: v_pair[par][:, k, c, :], lambda k: pt_pair[:, k, :, c, :],
                                   c == 0, c == KC - 1)
                last.then_inc(pv_done, 1)

            def project_out(n, heads):
                if heads[0] == 0:
                    pe.wait_ge(o_lo, n + 1)
                    pe.wait_ge(w_lo, (n // B) * PIECES + PIECES)
                at = group_at(n) + WWO
                for h in heads:
                    last = product(pe, misc_ps, lambda k: o_pair[:, k, h, :],
                                   lambda k: w_pair[:, k, ds(at + h * HID, HID)], h == 0, h == REP - 1)
                if heads[-1] == REP - 1:
                    last.then_inc(wo_done, 1)

            def step(n, par, x=True, w=True, nxt=True):
                first = isinstance(n, int) and n == 0
                scores(n, 0)
                scores(n, 1)
                if not first:
                    transpose_p(n - 1, 3)
                if nxt:
                    project_kv(n + 1, 1 - par)
                    project_q(n + 1, 1 - par)
                scores(n, 2)
                if not first:
                    values(n - 1, 1 - par, nxt)
                transpose_p(n, 0)
                scores(n, 3)
                if nxt:
                    transpose_q(n + 1)
                    transpose_cached_k(n + 1, 1 - par)
                    transpose_new_k(n + 1, 1 - par)
                transpose_p(n, 1)
                if not first:
                    project_out(n - 1, (0, 1, 2))
                transpose_p(n, 2)
                if not first:
                    project_out(n - 1, (3,))

            pe.wait_ge(s_const, 48)
            project_kv(0, 0)
            project_q(0, 0)
            transpose_cached_k(0, 0)
            transpose_new_k(0, 0)
            transpose_q(0)
            steps(pe, step)
            transpose_p(NT - 1, 3)
            values(NT - 1, 1, False)
            project_out(NT - 1, range(REP))

            def transpose4(bank, src):
                for c in range(DC):
                    last = pe.transpose(bank[:, c * P:(c + 1) * P], src[:, c * P:(c + 1) * P], ident[:])
                return last

            def linear(dst, xt, w, stop):
                for c in range(DC):
                    last = product(pe, dst, lambda k: xt[:, k, c, :], lambda k: w[:, k, c, :], c == 0,
                                   stop and c == DC - 1)
                return last

            def x1_transpose(b):
                pe.wait_ge(x1_done, b + 1)
                transpose4(banks[:, 0, :], x1_sb).then_inc(x1t_done, 1)

            def lora1(b):
                pe.wait_ge(x1t_lo, b + 1)
                pe.wait_ge(a1_lo, b + 1)
                for c in range(DC):
                    last = product(pe, banks[:, 1, 0:P], lambda k: a1_pair[:, k, c, :], lambda k: x1t_pair[:, k, c, :],
                                   c == 0, c == DC - 1)
                last.then_inc(low_done, 1)

            def block1(b):
                linear(banks[:, 2, :], x1t_pair, w1_pair, False)
                pe.wait_ge(low_lo, b + 1)
                product(pe, banks[:, 2, :], lambda k: low_pair[:, k, :], lambda k: b1_pair[:, k, :],
                        False, True).then_inc(y1_done, 1)

            def x2_transpose(b):
                pe.wait_ge(x2_done, b + 1)
                transpose4(banks[:, 3, :], x2_sb).then_inc(x2t_done, 1)

            def tokens(half):
                return slice(half * HT, (half + 1) * HT)

            def gate_up_lora(half, k, bank=tg_ps):
                if half == 0:
                    pe.wait_ge(ga_lo, k + 1)
                    pe.wait_ge(x3t_lo, HB)
                elif k == 0:
                    pe.wait_ge(x3t_lo, B)
                else:
                    pe.wait_ge(tg_own, 2 * half + k)
                for c in range(DC):
                    last = product(pe, bank, lambda j: ga_pair[k][:, j, c, :], lambda j: x3t_pair[:, j, c, tokens(half)],
                                   c == 0, c == DC - 1)
                last.then_inc(tg_done, 1)

            def stage(b, nxt=True, after=True):
                pe.wait_ge(x2t_lo, b + 1)
                linear(banks[:, 4, 0:E + ER], x2t_pair, ra_pair, True).then_inc(hl_done, 1)
                if nxt:
                    lora1(b + 1)
                    block1(b + 1)
                else:
                    linear(banks[:, 6, :], x2t_pair, w2_pair, False)
                    gate_up_lora(0, 0, banks[:, 0, :])
                pe.wait_ge(gates, GSTEPS * b + GSTEPS)
                pe.transpose(banks[:, 5, 0:P], hg[:].rearrange("p e r -> p (e r)"), ident[:]).then_inc(hgt_done, 1)
                if nxt:
                    pe.wait_ge(w2_lo, 1)
                    linear(banks[:, 6, :], x2t_pair, w2_pair, False)
                    x2_transpose(b + 1)
                else:
                    gate_up_lora(0, 1, banks[:, 1, :])
                pe.wait_ge(hgt_lo, b + 1)
                product(pe, banks[:, 6, :], lambda k: hgt_pair[:, k, :], lambda k: b2_pair[:, k, :],
                        False, True).then_inc(y2_done, 1)
                if after:
                    x1_transpose(b + 2)
                pe.wait_ge(x3_done, b + 1)
                transpose4(banks[:, 7, :], x3_sb).then_inc(x3t_done, 1)

            x1_transpose(0)
            lora1(0)
            pe.wait_ge(w1_lo, 1)
            pe.wait_ge(b1_lo, 1)
            block1(0)
            x2_transpose(0)
            x1_transpose(1)
            pe.wait_ge(sm_lo, 1)
            with pe.Fori(0, B - 2) as b:
                stage(b)
            stage(B - 2, after=False)
            stage(B - 1, nxt=False, after=False)

            def gate_up(half, m, par):
                pe.wait_ge(gu_lo, m + 1)
                for k, dst, at, at_b, sem_read, sem_done in ((0, g_ps, F_GATE, F_GATE_B, gsig_done, g_done),
                                                             (1, u_ps, F_UP, F_UP_B, act_done, u_done)):
                    if not (isinstance(m, int) and m == 0):
                        pe.wait_ge(sem_read, m)
                    for c in range(DC):
                        product(pe, dst, lambda j: fw_pair[par][:, j, at + c * P:at + (c + 1) * P],
                                lambda j: x3t_pair[:, j, c, tokens(half)], c == 0, False)
                    if isinstance(m, int) and m == half * FT:
                        pe.wait_ge(tg_lo, 2 * half + k + 1)
                    product(pe, dst, lambda j: fw_pair[par][:, j, at_b:at_b + P], lambda j: tg_pair[k][:, j, :],
                            False, True).then_inc(sem_done, 1)

            def down(m, par, start=False, stop=False):
                pe.wait_ge(dn_lo, m + 1)
                pe.wait_ge(act_lo, m + 1)
                if isinstance(m, int) and m == 0:
                    pe.wait_ge(tg_own, 2)
                if isinstance(m, int) and m == FT:
                    pe.wait_ge(ffn_added, HB)
                    pe.wait_ge(td_own, 1)
                last = product(pe, t_ps, lambda k: fw_pair[par][:, k, F_DOWN_A:FW], lambda k: act_pair[par][:, k, :],
                               start, stop)
                if stop:
                    last.then_inc(td_done, 1)
                for j in range(HB):
                    last = product(pe, ffn_bank[j], lambda k: act_pair[par][:, k, j * S:(j + 1) * S],
                                   lambda k: fw_pair[par][:, k, F_DOWN:F_DOWN_A], start, False)
                last.then_inc(down_done, 1)

            def down_lora(half):
                pe.wait_ge(td_lo, half + 1)
                for j in range(HB):
                    product(pe, ffn_bank[j], lambda k: td_pair[:, k, j * S:(j + 1) * S], lambda k: db_pair[:, k, :],
                            False, True).then_inc(ffn_done, 1)

            def ff_tiles(half):
                def ff_step(ft, par):
                    gate_up(half, half * FT + ft, par)
                    down(half * FT + ft - 1, 1 - par, start=isinstance(ft, int) and ft == 1)

                tiles(pe, half, ff_step)

            gate_up(0, 0, 0)
            ff_tiles(0)
            gate_up_lora(1, 0)
            down(FT - 1, (FT - 1) % 2, stop=True)
            gate_up_lora(1, 1)
            gate_up(1, FT, FT % 2)
            pe.wait_ge(db_lo, 1)
            down_lora(0)
            ff_tiles(1)
            down(2 * FT - 1, 1, stop=True)
            down_lora(1)


def rope_rows():
    inv = (1.0 / 10000.0 ** (np.arange(0, D, 2, dtype=np.float64) / D)).astype(np.float32)
    pos = np.arange(POS_END - 1 + S, dtype=np.float32)
    angle = (pos[:, None] * inv[None, :]).astype(np.float64)
    return np.concatenate([np.cos(angle), np.sin(angle)], 1).astype(np.float32)


def kernel(**inputs):
    import concourse.bacc as _bacc
    from concourse.bass_utils import run_bass_kernel_spmd as _run

    i = {k: np.asarray(v) for k, v in inputs.items()}
    x = i["x"]

    def by_partition(w, cols):
        return w.reshape(cols, DC, P).transpose(2, 1, 0)

    wq = i["L0_cond_Wq"].reshape(HK, REP * D, DC, P).transpose(0, 3, 2, 1).reshape(HK, P, -1)
    wk = i["L0_cond_Wk"].reshape(HK, D, DC, P).transpose(0, 3, 2, 1)
    wv = i["L0_cond_Wv"].reshape(HK, D, DC, P).transpose(0, 3, 2, 1)
    wkv = np.stack([wk, wv], 3).reshape(HK, P, -1)
    wo = i["L0_cond_Wo"].reshape(HID, HK, REP, D).transpose(1, 3, 2, 0).reshape(HK, P, -1)
    w_att = np.concatenate([wq, wkv, wo], 2).reshape(HK, P, PIECES, PW).transpose(0, 2, 1, 3).reshape(NT, P, PW)
    kv = np.stack([i["L0_cond_k_cache"], i["L0_cond_v_cache"]], 3)
    kv = kv.transpose(2, 0, 1, 3, 4).reshape(HK, PAGES, PSIZE, 2 * D)
    arrays = {
        "x": x,
        "xT": x.reshape(B, S, DC, P).transpose(0, 3, 2, 1).reshape(B, P, DC * S),
        "w_att": w_att,
        "kv": kv,
        "wnorm": np.stack([i["L0_cond_q_norm_w"], i["L0_cond_k_norm_w"]]),
        "pages": i["itok_Bx16_0_63"],
        "seqlens": i["itok_B_207_1644"],
        "trig": rope_rows(),
        "ident": np.eye(P, dtype=np.float32),
        "iota": np.arange(CACHE, dtype=np.float32),
    }
    w12 = np.stack([by_partition(i[k], HID).reshape(P, -1) for k in ("L1_cond_weight", "L2_cond_W")])
    ra = np.concatenate([by_partition(i["L2_cond_Wr"], E), by_partition(i["L2_cond_A"].reshape(ER, HID), ER)], 2)

    def padded(a, axis):
        wide = [(0, 0)] * a.ndim
        wide[axis] = (0, FP - F)
        return np.pad(a, wide)

    gate_w, up_w = (padded(i[k], 0).reshape(FT, P, DC, P).transpose(0, 3, 2, 1).reshape(FT, P, DC * P)
                    for k in ("L3_cond_W_gate", "L3_cond_W_up"))
    down_w = padded(i["L3_cond_W_down"], 1).reshape(HID, FT, P).transpose(1, 2, 0)
    arrays.update({
        "w12": w12,
        "a1": i["L1_cond_lora_A"].reshape(-1, DC, P, R1).transpose(0, 2, 1, 3).reshape(-1, P, DC * R1),
        "b1": i["L1_cond_lora_B_w"].T,
        "ra": ra.reshape(P, -1),
        "b2": i["L2_cond_B"].transpose(0, 2, 1).reshape(ER, HID),
        "label": i["itok_B_0_4"], "lang": i["itok_B_0_7"], "lora": i["itok_B_2_6"],
        "experts": np.arange(E, dtype=np.float32),
        "lower": np.tril(np.ones((E, E), np.float32), -1).reshape(-1),
        "own": np.kron(np.eye(B), np.full((R3, 1), LORA3_SCALE)).astype(np.float32),
        "gu_a": np.stack([i[k][0].reshape(-1, R3, DC, P).transpose(0, 3, 2, 1).reshape(-1, P, DC * R3)
                          for k in ("L3_cond_A_gate", "L3_cond_A_up")]),
        "gu_b": np.stack([padded(i[k][0], 1).transpose(0, 2, 1) for k in ("L3_cond_B_gate", "L3_cond_B_up")]),
        "d_a": padded(i["L3_cond_A_down"][0], 2).reshape(-1, R3, FT, P).transpose(0, 3, 2, 1),
        "d_b": i["L3_cond_B_down"][0].transpose(0, 2, 1),
        "fw": np.stack([gate_w, up_w, down_w]),
    })
    nc = _bacc.Bacc("TRN2", target_bir_lowering=False, num_devices=1)
    arrays = {k: np.ascontiguousarray(v) for k, v in arrays.items()}
    t = {k: nc.dram_tensor(f"in_{k}", v.shape, mybir.dt.from_np(v.dtype), kind="ExternalInput").ap()
         for k, v in arrays.items()}
    out = nc.dram_tensor("out_x", (B, S, HID), F32, kind="ExternalOutput").ap()
    build(nc, t, out)
    r = _run(nc, [{f"in_{k}": v for k, v in arrays.items()}], core_ids=[0])
    return r.results[0]["out_x"]
```
